# Optimizing a Trainium2 kernel written in Bass

```python
import numpy as np
import jax
import jax.numpy as jnp

def _softmax(x, axis=-1):
    return jax.nn.softmax(x, axis=axis)

def _gelu(x):
    return jax.nn.gelu(x, approximate=True)

def _silu(x):
    return jax.nn.silu(x)

def _sigmoid(x):
    return jax.nn.sigmoid(x)

def _layernorm(x, axis=-1, eps=1e-05):
    m = jnp.mean(x, axis=axis, keepdims=True)
    v = jnp.var(x, axis=axis, keepdims=True)
    return (x - m) / jnp.sqrt(v + eps)

def _scatter_add(tgt, idx, src, axis=0):
    return tgt.at[idx].add(src)

def _segment_sum(src, seg, n):
    return jax.ops.segment_sum(src, seg, n)
kernel_name = 'mk_recurrent_d1_jaxref_r8_af2b8f'

def setup_inputs(seed: int=0):
    np.random.seed(seed)
    _w = jnp.asarray

    def _L0_attn_setup():
        import jax, jax.numpy as jnp
        import numpy as np
        from jax import lax
        H = 16
        D = 128
        HID = 256
        CONV_K = 4
        CHUNK = 64
        EPS = 1e-06

        def silu(x):
            return x * jax.nn.sigmoid(x)

        def short_conv(x, w):
            B, T, C = x.shape
            K = w.shape[1]
            xp = jnp.pad(x, ((0, 0), (K - 1, 0), (0, 0)))
            y = sum((xp[:, j:j + T, :] * w[None, None, :, j] for j in range(K)))
            return silu(y)

        def l2norm(x):
            return x * lax.rsqrt(jnp.sum(x * x, -1, keepdims=True) + EPS)

        def rmsnorm(x, w):
            return x * lax.rsqrt(jnp.mean(x * x, -1, keepdims=True) + EPS) * w

        def kda_scan(q, k, v, g, beta):
            B, T, _, _ = q.shape
            NC = T // CHUNK

            def tm(a):
                a = jnp.moveaxis(a, 1, 0)
                return a.reshape((NC, CHUNK) + a.shape[1:])

            def step(S, inp):
                qt, kt, vt, gt, bt = inp
                S = S * jnp.exp(gt)[..., :, None]
                u = (vt - jnp.einsum('bhk,bhkv->bhv', kt, S)) * bt[..., None]
                S = S + kt[..., None] * u[..., None, :]
                ot = jnp.einsum('bhk,bhkv->bhv', qt, S)
                return (S, ot)

            @jax.checkpoint
            def chunk_body(S, inp):
                return lax.scan(step, S, inp)
            S0 = jnp.zeros((B, H, D, D), dtype=q.dtype)
            _, o = lax.scan(chunk_body, S0, (tm(q), tm(k), tm(v), tm(g), tm(beta)))
            o = o.reshape(T, B, H, D)
            return jnp.moveaxis(o, 0, 1)
        key = jax.random.key(seed)
        ks = jax.random.split(key, 16)
        s_h = 1.0 / np.sqrt(HID)
        s_d = 1.0 / np.sqrt(D)
        inp = {'hidden_states': jax.random.normal(ks[0], (2, 512, HID), dtype=jnp.float32), 'Wq': jax.random.normal(ks[1], (HID, H * D), dtype=jnp.float32) * s_h, 'Wk': jax.random.normal(ks[2], (HID, H * D), dtype=jnp.float32) * s_h, 'Wv': jax.random.normal(ks[3], (HID, H * D), dtype=jnp.float32) * s_h, 'conv_q_w': jax.random.normal(ks[4], (H * D, CONV_K), dtype=jnp.float32) * 0.5, 'conv_k_w': jax.random.normal(ks[5], (H * D, CONV_K), dtype=jnp.float32) * 0.5, 'conv_v_w': jax.random.normal(ks[6], (H * D, CONV_K), dtype=jnp.float32) * 0.5, 'A_log': jnp.log(jax.random.uniform(ks[7], (1, 1, H, 1), dtype=jnp.float32, minval=1.0, maxval=16.0)), 'Wfa': jax.random.normal(ks[8], (HID, D), dtype=jnp.float32) * s_h, 'Wfb': jax.random.normal(ks[9], (D, H * D), dtype=jnp.float32) * s_d, 'dt_bias': jax.random.normal(ks[10], (H * D,), dtype=jnp.float32) * 0.5, 'Wb': jax.random.normal(ks[11], (HID, H), dtype=jnp.float32) * s_h, 'Wga': jax.random.normal(ks[12], (HID, D), dtype=jnp.float32) * s_h, 'Wgb': jax.random.normal(ks[13], (D, H * D), dtype=jnp.float32) * s_d, 'o_norm_w': jnp.ones((D,), dtype=jnp.float32), 'Wo': jax.random.normal(ks[14], (H * D, HID), dtype=jnp.float32) * s_h}
        return inp
    _L0_attn_in = _L0_attn_setup()

    def _L0_ffn_setup():
        import jax, jax.numpy as jnp
        import numpy as np
        H = 256
        E = 64
        I = 64
        SI = 64
        TOP_K = 8
        B, T = (2, 64)
        key = jax.random.key(seed)
        ks = jax.random.split(key, 8)
        s = 0.02
        return {'h': jax.random.normal(ks[0], (B, T, H), jnp.float32), 'gate_w': jax.random.normal(ks[1], (E, H), jnp.float32) * s, 'gu_w': jax.random.normal(ks[2], (E, 2 * I, H), jnp.float32) * s, 'dp_w': jax.random.normal(ks[3], (E, H, I), jnp.float32) * s, 'sh_gate_w': jax.random.normal(ks[4], (SI, H), jnp.float32) * s, 'sh_up_w': jax.random.normal(ks[5], (SI, H), jnp.float32) * s, 'sh_down_w': jax.random.normal(ks[6], (H, SI), jnp.float32) * s, 'sh_gate1_w': jax.random.normal(ks[7], (1, H), jnp.float32) * s}
    _L0_ffn_in = _L0_ffn_setup()
    _d = {'L0_attn_hidden_states': _L0_attn_in['hidden_states'], 'L0_attn_Wq': _L0_attn_in['Wq'], 'L0_attn_Wk': _L0_attn_in['Wk'], 'L0_attn_Wv': _L0_attn_in['Wv'], 'L0_attn_conv_q_w': _L0_attn_in['conv_q_w'], 'L0_attn_conv_k_w': _L0_attn_in['conv_k_w'], 'L0_attn_conv_v_w': _L0_attn_in['conv_v_w'], 'L0_attn_A_log': _L0_attn_in['A_log'], 'L0_attn_Wfa': _L0_attn_in['Wfa'], 'L0_attn_Wfb': _L0_attn_in['Wfb'], 'L0_attn_dt_bias': _L0_attn_in['dt_bias'], 'L0_attn_Wb': _L0_attn_in['Wb'], 'L0_attn_Wga': _L0_attn_in['Wga'], 'L0_attn_Wgb': _L0_attn_in['Wgb'], 'L0_attn_o_norm_w': _L0_attn_in['o_norm_w'], 'L0_attn_Wo': _L0_attn_in['Wo'], 'L0_ffn_gate_w': _L0_ffn_in['gate_w'], 'L0_ffn_gu_w': _L0_ffn_in['gu_w'], 'L0_ffn_dp_w': _L0_ffn_in['dp_w'], 'L0_ffn_sh_gate_w': _L0_ffn_in['sh_gate_w'], 'L0_ffn_sh_up_w': _L0_ffn_in['sh_up_w'], 'L0_ffn_sh_down_w': _L0_ffn_in['sh_down_w'], 'L0_ffn_sh_gate1_w': _L0_ffn_in['sh_gate1_w']}
    _x0 = _d['L0_attn_hidden_states']
    _d['L0_attn_hidden_states'] = jax.random.normal(jax.random.fold_in(jax.random.key(seed), 1), (2, 512, 256), dtype=_x0.dtype)
    del _x0
    return _d

def reference(L0_attn_hidden_states, L0_attn_Wq, L0_attn_Wk, L0_attn_Wv, L0_attn_conv_q_w, L0_attn_conv_k_w, L0_attn_conv_v_w, L0_attn_A_log, L0_attn_Wfa, L0_attn_Wfb, L0_attn_dt_bias, L0_attn_Wb, L0_attn_Wga, L0_attn_Wgb, L0_attn_o_norm_w, L0_attn_Wo, L0_ffn_gate_w, L0_ffn_gu_w, L0_ffn_dp_w, L0_ffn_sh_gate_w, L0_ffn_sh_up_w, L0_ffn_sh_down_w, L0_ffn_sh_gate1_w):

    def _L0_attn_ref(hidden_states, Wq, Wk, Wv, conv_q_w, conv_k_w, conv_v_w, A_log, Wfa, Wfb, dt_bias, Wb, Wga, Wgb, o_norm_w, Wo):
        import jax, jax.numpy as jnp
        import numpy as np
        from jax import lax
        H = 16
        D = 128
        HID = 256
        CONV_K = 4
        CHUNK = 64
        EPS = 1e-06

        def silu(x):
            return x * jax.nn.sigmoid(x)

        def short_conv(x, w):
            B, T, C = x.shape
            K = w.shape[1]
            xp = jnp.pad(x, ((0, 0), (K - 1, 0), (0, 0)))
            y = sum((xp[:, j:j + T, :] * w[None, None, :, j] for j in range(K)))
            return silu(y)

        def l2norm(x):
            return x * lax.rsqrt(jnp.sum(x * x, -1, keepdims=True) + EPS)

        def rmsnorm(x, w):
            return x * lax.rsqrt(jnp.mean(x * x, -1, keepdims=True) + EPS) * w

        def kda_scan(q, k, v, g, beta):
            B, T, _, _ = q.shape
            NC = T // CHUNK

            def tm(a):
                a = jnp.moveaxis(a, 1, 0)
                return a.reshape((NC, CHUNK) + a.shape[1:])

            def step(S, inp):
                qt, kt, vt, gt, bt = inp
                S = S * jnp.exp(gt)[..., :, None]
                u = (vt - jnp.einsum('bhk,bhkv->bhv', kt, S)) * bt[..., None]
                S = S + kt[..., None] * u[..., None, :]
                ot = jnp.einsum('bhk,bhkv->bhv', qt, S)
                return (S, ot)

            @jax.checkpoint
            def chunk_body(S, inp):
                return lax.scan(step, S, inp)
            S0 = jnp.zeros((B, H, D, D), dtype=q.dtype)
            _, o = lax.scan(chunk_body, S0, (tm(q), tm(k), tm(v), tm(g), tm(beta)))
            o = o.reshape(T, B, H, D)
            return jnp.moveaxis(o, 0, 1)
        B, T, _ = hidden_states.shape
        q = short_conv(hidden_states @ Wq, conv_q_w)
        k = short_conv(hidden_states @ Wk, conv_k_w)
        v = short_conv(hidden_states @ Wv, conv_v_w)
        g = (hidden_states @ Wfa @ Wfb).reshape(B, T, H, D)
        g = -jnp.exp(A_log) * jax.nn.softplus(g + dt_bias.reshape(1, 1, H, D))
        beta = jax.nn.sigmoid(hidden_states @ Wb)
        q = l2norm(q.reshape(B, T, H, D)) * D ** (-0.5)
        k = l2norm(k.reshape(B, T, H, D))
        v = v.reshape(B, T, H, D)
        o = kda_scan(q, k, v, g, beta)
        go = (hidden_states @ Wga @ Wgb).reshape(B, T, H, D)
        o = rmsnorm(o, o_norm_w) * jax.nn.sigmoid(go)
        o = o.reshape(B, T, H * D) @ Wo
        return o

    def _L0_ffn_ref(h, gate_w, gu_w, dp_w, sh_gate_w, sh_up_w, sh_down_w, sh_gate1_w):
        import jax, jax.numpy as jnp
        import numpy as np
        H = 256
        E = 64
        I = 64
        SI = 64
        TOP_K = 8
        B, T = (2, 64)
        Bb, Tt, Hh = h.shape
        x = h.reshape(Bb * Tt, Hh)
        N = x.shape[0]
        logits = x @ gate_w.T
        topv, topi = jax.lax.top_k(logits, TOP_K)
        rw = jax.nn.softmax(topv.astype(jnp.float32), axis=-1).astype(x.dtype)
        W = jnp.zeros((N, E), x.dtype).at[jnp.arange(N)[:, None], topi].set(rw)
        gu = jnp.einsum('nh,eih->nei', x, gu_w)
        gate, up = (gu[..., :I], gu[..., I:])
        inter = jax.nn.silu(gate) * up
        inter_w = inter * W[:, :, None]
        out = jnp.einsum('nei,ehi->nh', inter_w, dp_w)
        sh_inter = jax.nn.silu(x @ sh_gate_w.T) * (x @ sh_up_w.T)
        sh_out = sh_inter @ sh_down_w.T
        sh_g = jax.nn.sigmoid(x @ sh_gate1_w.T)
        out = out + sh_g * sh_out
        return out.reshape(Bb, Tt, Hh)
    x = L0_attn_hidden_states
    xn = _layernorm(x, axis=-1)
    s = _L0_attn_ref(xn, L0_attn_Wq, L0_attn_Wk, L0_attn_Wv, L0_attn_conv_q_w, L0_attn_conv_k_w, L0_attn_conv_v_w, L0_attn_A_log, L0_attn_Wfa, L0_attn_Wfb, L0_attn_dt_bias, L0_attn_Wb, L0_attn_Wga, L0_attn_Wgb, L0_attn_o_norm_w, L0_attn_Wo)
    g = _silu(_L0_ffn_ref(xn, L0_ffn_gate_w, L0_ffn_gu_w, L0_ffn_dp_w, L0_ffn_sh_gate_w, L0_ffn_sh_up_w, L0_ffn_sh_down_w, L0_ffn_sh_gate1_w))
    x = x + s * g
    return x

_drawn_inputs = setup_inputs


def setup_inputs(seed=0):
    import zlib

    import numpy as np

    out = dict(_drawn_inputs(seed))
    spreads = {'L0_attn_o_norm_w': (1.0, 0.6)}
    factors = {'L0_attn_Wq': 8.0,
     'L0_attn_Wk': 8.0,
     'L0_attn_Wv': 8.0,
     'L0_attn_conv_q_w': 8.0,
     'L0_attn_conv_k_w': 8.0,
     'L0_attn_conv_v_w': 8.0,
     'L0_attn_A_log': 8.0,
     'L0_attn_Wfa': 8.0,
     'L0_attn_Wfb': 8.0,
     'L0_attn_dt_bias': 8.0,
     'L0_attn_Wb': 8.0,
     'L0_attn_Wga': 8.0,
     'L0_attn_Wgb': 8.0,
     'L0_attn_Wo': 8.0,
     'L0_ffn_gate_w': 8.0,
     'L0_ffn_gu_w': 8.0,
     'L0_ffn_dp_w': 8.0,
     'L0_ffn_sh_gate_w': 8.0,
     'L0_ffn_sh_up_w': 8.0,
     'L0_ffn_sh_down_w': 8.0,
     'L0_ffn_sh_gate1_w': 8.0}
    for name, (base, spread) in spreads.items():
        noise = np.random.default_rng([zlib.crc32(name.encode()), seed]).standard_normal(out[name].shape)
        drawn = base * np.exp(spread * noise) if base else spread * noise
        out[name] = jnp.asarray(drawn.astype(out[name].dtype))
    for name, factor in factors.items():
        out[name] = (out[name] * factor).astype(out[name].dtype)
    return out
```

```python
from contextlib import ExitStack

import numpy as np

import concourse.bass as bass
from concourse import mybir

F32 = mybir.dt.float32
U32 = mybir.dt.uint32
ACT = mybir.ActivationFunctionType
ALU = mybir.AluOpType
AX_X = mybir.AxisListType.X

P = 128
BATCH, SEQ, HID = 2, 512, 256
TOK = BATCH * SEQ
TT = TOK // P
HEADS, D = 16, 128
KT = HID // P
CH = 128
NC = SEQ // CH
LEV = 7
HALF = SEQ // 2
TAPS = 4
HC = 3 * TAPS + 2
EXPERTS, INNER, TOPK = 64, 64, 8
PAIRS = EXPERTS // 2
UNITS = HEADS * BATCH
NORM_EPS, LN_EPS = 1e-6, 1e-5
SMALL = 2.0 ** -6
NEG_BIG = -3.0e38
assert PAIRS == UNITS


def build(nc, x_in, wproj, wout, wab, wrouter, wshared, wsh_down, wgu, wdown, o_norm, consts,
          masks, beta_dram, route_dram, out):
    with ExitStack() as ctx:
        def sb(name, *shape, dt=F32):
            return ctx.enter_context(nc.sbuf_tensor(name, [shape[0], *shape[1:]], dt))

        def sem(name):
            return ctx.enter_context(nc.semaphore(name))

        xT = sb("xT", P, KT, TOK)
        fa = sb("fa", P, TOK)
        ga = sb("ga", P, TOK)
        s_acc = sb("s_acc", P, TT, HID)
        f_acc = sb("f_acc", P, TT, HID)
        ident = sb("ident", P, P)
        ident4 = sb("ident4", P, NC, P)
        ones = sb("ones", P, P)
        mask = sb("mask", P, LEV, HALF)
        onorm = sb("onorm", P, 1)
        biases = sb("biases", P, 4)
        wpc = sb("wpc", P, 8 * P + HC)
        wp = wpc[:, 0:8 * P].rearrange("p (n c) -> p n c", c=P)
        taps = wpc[:, 8 * P:8 * P + 3 * TAPS].rearrange("p (n j) -> p n j", j=TAPS)
        dtb = wpc[:, 8 * P + 3 * TAPS:8 * P + 3 * TAPS + 1]
        a_log = wpc[:, 8 * P + 3 * TAPS + 1:8 * P + HC]
        exp_a = sb("exp_a", P, 1)
        wo = sb("wo", P, HID)
        gu = sb("gu", P, KT, 2, P)
        dw = sb("dw", P, HID)
        wbc = sb("wbc", P, TOK)
        bb = sb("bb", P, SEQ)
        KL = sb("KL", P, LEV, SEQ)
        KQL = sb("KQL", P, LEV, 2, HALF)
        kn = sb("kn", P, SEQ)
        qn = sb("qn", P, SEQ)
        kb = sb("kb", P, SEQ)
        vb = sb("vb", P, SEQ)
        kbG = sb("kbG", P, SEQ)
        qG = sb("qG", P, SEQ)
        kS = sb("kS", P, SEQ)
        dec = sb("dec", P, BATCH, NC)
        gate = sb("gate", P, BATCH, SEQ)
        raw = [sb(f"raw{n}", P, SEQ) for n in "qkv"]
        act = [sb(f"act{n}", P, SEQ) for n in "qkv"]
        sq = [sb(f"sq{n}", P, SEQ) for n in "qk"]
        rn = [sb(f"rn{n}", P, SEQ) for n in "qk"]
        absz = sb("absz", P, SEQ)
        relz = sb("relz", P, SEQ)
        ez = sb("ez", P, SEQ)
        lz = sb("lz", P, SEQ)
        hz = sb("hz", P, SEQ)
        small = sb("small", P, SEQ, dt=U32)
        pre = sb("pre", P, SEQ)
        suf = sb("suf", P, SEQ)
        zero = sb("zero", P, SEQ)
        F = sb("F", P, LEV, SEQ)
        Fpre = sb("Fpre", P, SEQ)
        Fsuf = sb("Fsuf", P, SEQ)
        Pt = sb("Pt", P, SEQ)
        Bt = sb("Bt", P, LEV, SEQ)
        T = sb("T", P, NC, P)
        Tt = sb("Tt", P, NC, P)
        W = sb("W", P, NC, P)
        kStok = sb("kStok", P, NC, P)
        vbT = sb("vbT", P, NC, P)
        R = sb("R", P, 2, P)
        U = sb("U", P, 2, P)
        S = sb("S", P, 2, P)
        osq = sb("osq", P, SEQ)
        orn = sb("orn", P, SEQ)
        ogw = sb("ogw", P, SEQ)
        osc = sb("osc", P, SEQ)
        sg = sb("sg", P, 2, SEQ)
        hh = sb("hh", P, 2, SEQ)
        hw = sb("hw", P, 2, SEQ)

        LV = [ctx.enter_context(nc.psum_tensor(f"LV{n}", [P, 512], F32)) for n in range(2)]
        IA = ctx.enter_context(nc.psum_tensor("IA", [P, 512], F32))
        IB = ctx.enter_context(nc.psum_tensor("IB", [P, 512], F32))
        OX = ctx.enter_context(nc.psum_tensor("OX", [P, 512], F32))
        FB = [ctx.enter_context(nc.psum_tensor(f"FB{n}", [P, 512], F32)) for n in range(3)]

        PER = {}

        def unit_sem(name, per=1):
            s = sem(name)
            PER[id(s)] = per
            keep.append(s)
            return s

        keep = []

        def after(eng, s, u, k=None):
            per = PER[id(s)]
            v = u * per + (per if k is None else k)
            if not isinstance(v, int) or v > 0:
                eng.wait_ge(s, v)

        d_const = sem("d_const")
        d_x = sem("d_x")
        d_pw = sem("d_pw")
        d_scr = sem("d_scr")
        d_out = sem("d_out")
        d_wp = sem("d_wp")
        d_wo = sem("d_wo")
        d_gu = sem("d_gu")
        d_dw = sem("d_dw")
        d_wbc = sem("d_wbc")
        d_bb = sem("d_bb")
        pro_v = sem("pro_v")
        pro_a = sem("pro_a")
        pro_p = sem("pro_p")
        end_v = sem("end_v")
        end_a = sem("end_a")

        m_g, m_go, m_q, m_k, m_v, m_nq, m_nk = [unit_sem(n) for n in
            ("m_g", "m_go", "m_q", "m_k", "m_v", "m_nq", "m_nk")]
        m_gate = unit_sem("m_gate", 2)
        m_up = unit_sem("m_up", 2)
        m_down = unit_sem("m_down", 4)
        m_lv = unit_sem("m_lv", LEV + 1)
        m_tr = unit_sem("m_tr", 3)
        m_w = unit_sem("m_w", 2 * (LEV - 1))
        m_t = unit_sem("m_t", 2 * (LEV - 1))
        m_r = unit_sem("m_r", NC - 1)
        m_u = unit_sem("m_u", NC)
        m_s = unit_sem("m_s", NC - 1)
        m_o = unit_sem("m_o", NC)
        m_ss = unit_sem("m_ss")
        m_wo = unit_sem("m_wo", 2)
        v_lv = unit_sem("v_lv", LEV + 1)
        v_t = unit_sem("v_t", 2 * LEV)
        v_sp = unit_sem("v_sp", 8)
        v_conv = [unit_sem(f"v_conv{n}", TAPS - 1) for n in "qkv"]
        v_norm = [unit_sem(f"v_norm{n}") for n in "qk"]
        v_prod = unit_sem("v_prod", LEV)
        v_full = unit_sem("v_full")
        v_r = unit_sem("v_r", NC - 1)
        v_s = unit_sem("v_s", NC - 1)
        v_h = unit_sem("v_h", 2)
        v_f = unit_sem("v_f", 4)
        v_og = unit_sem("v_og")
        v_osc = unit_sem("v_osc")
        v_sacc = unit_sem("v_sacc", 2)
        a_abs = unit_sem("a_abs", 2)
        a_e = unit_sem("a_e")
        a_ln = unit_sem("a_ln")
        a_gate = unit_sem("a_gate")
        a_tap = [unit_sem(f"a_tap{n}") for n in "qkv"]
        a_silu = [unit_sem(f"a_silu{n}") for n in "qkv"]
        a_nln = [unit_sem(f"a_nln{n}") for n in "qk"]
        a_rn = [unit_sem(f"a_rn{n}") for n in "qk"]
        a_F = unit_sem("a_F", LEV)
        a_full = unit_sem("a_full")
        a_tr = unit_sem("a_tr", 2)
        a_w = unit_sem("a_w", 2 * (LEV - 1))
        a_u = unit_sem("a_u", NC)
        a_sg = unit_sem("a_sg", 2)
        a_osq = unit_sem("a_osq")
        a_oln = unit_sem("a_oln")
        a_orn = unit_sem("a_orn")
        p_sq = [unit_sem(f"p_sq{n}") for n in "qk"]
        p_zero = unit_sem("p_zero")
        p_sum = unit_sem("p_sum", 2 * LEV)
        p_kb = unit_sem("p_kb")
        p_vb = unit_sem("p_vb")
        p_h = unit_sem("p_h", 2)

        def halves(ap, s):
            return ap.rearrange("p (n two s) -> p n two s", two=2, s=s)

        def c4(ap):
            return ap.rearrange("p (c n) -> p c n", c=NC)

        NCONST = 9 * 16
        PA_RSTD, PA_XT, PA_FAGA, PA_BETA = 2, 6, 10, 12
        PA_SGATE, PA_EXPR, PA_ROUTE = 16, 17, 19

        def sh_h(t):
            return sh_hidden[0:INNER, t * P:(t + 1) * P]

        def route_tok(t):
            return routed[:, t, :]

        sh_hidden = Bt[:, 0:2, :].rearrange("p a b -> p (a b)")
        sh_silu = Bt[:, 2:4, :].rearrange("p a b -> p (a b)")
        logits = Bt[:, 4, :].rearrange("p (t e) -> p t e", e=EXPERTS)
        lmask = Bt[:, 5, :].rearrange("p (t e) -> p t e", e=EXPERTS)
        routed = Bt[:, 6, :].rearrange("p (t e) -> p t e", e=EXPERTS)
        shg = R[:, 0, 0:TT]
        top8 = R[:, 1, 0:TT * 8].rearrange("p (t e) -> p t e", e=8)
        ntop = R[:, 1, 64:64 + TT]
        rsum = R[:, 1, 72:72 + TT]
        mean = R[:, 0, 8:8 + TT]
        var = R[:, 0, 16:16 + TT]
        rstd = R[:, 0, 24:24 + TT]
        PV_VAR, PV_XN, PV_SH, PV_ROUTE, PV_END = 5, 6, 8, 32, 38

        block = ctx.enter_context(nc.Block())

        @block.sync
        def _(sp):
            sp.dma_start(s_acc[:, :, :], x_in.rearrange("(t p) h -> p t h", p=P)).then_inc(d_x, 16)
            sp.dma_start(ident[:, :], consts[:, 0, :]).then_inc(d_const, 16)
            sp.dma_start(ones[:, :], consts[:, 1, :]).then_inc(d_const, 16)
            for c in range(NC):
                sp.dma_start(ident4[:, c, :], consts[:, 0, :]).then_inc(d_const, 16)
            sp.dma_start(mask[:, :, :], masks).then_inc(d_const, 16)
            sp.dma_start(onorm[:, :], o_norm).then_inc(d_const, 16)
            sp.dma_start(biases[:, :], consts[:, 2, 0:4]).then_inc(d_const, 16)
            sp.dma_start(F[:, 0, :].rearrange("p (k c) -> p k c", k=2), wab).then_inc(d_pw, 16)
            sp.dma_start(F[:, 1, 0:2 * (EXPERTS + 1)].rearrange("p (k c) -> p k c", k=2), wrouter).then_inc(d_pw, 16)
            sp.dma_start(F[:, 2, 0:2 * (P + HEADS)].rearrange("p (k c) -> p k c", k=2), wshared).then_inc(d_pw, 16)
            sp.dma_start(F[0:INNER, 3, 0:HID], wsh_down).then_inc(d_pw, 16)
            sp.dma_start(wpc[:, :], wproj[0:P, :]).then_inc(d_wp, 16)
            sp.wait_ge(pro_a, PA_BETA)
            sp.dma_start(beta_dram, KL[0:HEADS, 2:4, :].rearrange("p a b -> p (a b)")).then_inc(d_scr, 16)
            sp.wait_ge(pro_a, PA_ROUTE)
            sp.dma_start(route_dram, KL[0:EXPERTS, 0:2, :].rearrange("p a b -> p (a b)")).then_inc(d_scr, 16)
            sp.wait_ge(d_scr, 32)
            sp.dma_start(bb[:, :], beta_dram[0:1, 0:SEQ].to_broadcast([P, SEQ])).then_inc(d_bb, 16)

            def unit_loads(u, b, head, last):
                after(sp, m_up, u - 1)
                sp.dma_start(gu[:, :, :, :].rearrange("p k g c -> p (k g c)"),
                             wgu[bass.ds(u * P, P), :]).then_inc(d_gu, 16)
                after(sp, m_down, u - 1)
                sp.dma_start(dw[:, :], wdown[bass.ds(u * P, P), :]).then_inc(d_dw, 16)
                after(sp, p_h, u - 1)
                for e in range(2):
                    sp.dma_start(wbc[e * INNER:(e + 1) * INNER, :],
                                 route_dram[bass.ds(2 * u + e, 1), :].to_broadcast([INNER, TOK]))\
                        .then_inc(d_wbc, 16)
                if b == 0:
                    after(sp, m_wo, u - 1)
                    sp.dma_start(wo[:, :], wout[bass.ds(head * P, P), :]).then_inc(d_wo, 16)
                if not last:
                    after(sp, p_kb, u)
                    after(sp, p_vb, u)
                    nh = head if b == 0 else head + 1
                    sp.dma_start(bb[:, :], beta_dram[bass.ds(nh, 1), (1 - b) * SEQ:(2 - b) * SEQ]
                                 .to_broadcast([P, SEQ])).then_inc(d_bb, 16)
                    if b == 0:
                        after(sp, m_v, u + 1)
                        after(sp, v_conv[2], u + 1)
                        after(sp, v_sp, u + 1)
                        sp.dma_start(wpc[:, :], wproj[bass.ds((head + 1) * P, P), :]).then_inc(d_wp, 16)

            for b in range(BATCH):
                unit_loads(b, b, 0, False)
            with sp.Fori(1, HEADS - 1) as h:
                for b in range(BATCH):
                    unit_loads(2 * h + b, b, h, False)
            h = HEADS - 1
            for b in range(BATCH):
                u = 2 * h + b
                after(sp, m_up, u - 1)
                sp.dma_start(gu[:, :, :, :].rearrange("p k g c -> p (k g c)"),
                             wgu[u * P:(u + 1) * P, :]).then_inc(d_gu, 16)
                after(sp, m_down, u - 1)
                sp.dma_start(dw[:, :], wdown[u * P:(u + 1) * P, :]).then_inc(d_dw, 16)
                after(sp, p_h, u - 1)
                for e in range(2):
                    sp.dma_start(wbc[e * INNER:(e + 1) * INNER, :],
                                 route_dram[2 * u + e:2 * u + e + 1, :].to_broadcast([INNER, TOK])).then_inc(d_wbc, 16)
                if b == 0:
                    after(sp, m_wo, u - 1)
                    sp.dma_start(wo[:, :], wout[h * P:(h + 1) * P, :]).then_inc(d_wo, 16)
                    after(sp, p_kb, u)
                    after(sp, p_vb, u)
                    sp.dma_start(bb[:, :], beta_dram[h:h + 1, SEQ:2 * SEQ].to_broadcast([P, SEQ])).then_inc(d_bb, 16)
            after(sp, m_lv, UNITS - 1)
            sp.dma_start(KL[:, 0:4, :].rearrange("p a b -> p (a b)").rearrange("p (t h) -> p t h", t=TT),
                         x_in.rearrange("(t p) h -> p t h", p=P)).then_inc(d_x, 16)
            for t in range(4):
                sp.wait_ge(end_v, 2 * t + 2)
                sp.dma_start(out.rearrange("(t p) h -> p t h", p=P)[:, 2 * t:2 * t + 2, :],
                             s_acc[:, 2 * t:2 * t + 2, :]).then_inc(d_out, 16)
            sp.wait_ge(d_out, 64)

        @block.tensor
        def _(pe):
            mm = pe.matmul

            pe.wait_ge(d_const, NCONST)
            pe.wait_ge(pro_v, PV_XN)
            for q in range(4):
                bank = (LV + [IA, IB])[q]
                for t in range(2):
                    for k in range(KT):
                        m = pe.transpose(bank[:, (k * 2 + t) * P:(k * 2 + t + 1) * P],
                                         f_acc[:, 2 * q + t, k * P:(k + 1) * P], ident[:, :])
                m.then_inc(pro_p, 1)
            pe.wait_ge(pro_a, PA_XT)
            pe.wait_ge(d_pw, 64)
            wab_sb = F[:, 0, :].rearrange("p (k c) -> p k c", k=2)
            for n in range(2):
                for b in range(2):
                    bank = (FB + [OX])[2 * n + b]
                    for k in range(KT):
                        m = mm(bank[:, :], wab_sb[:, k, n * P:(n + 1) * P], xT[:, k, b * SEQ:(b + 1) * SEQ],
                               start=k == 0, stop=k == 1)
                    m.then_inc(pro_p, 1)
            wsh = F[:, 2, 0:2 * (P + HEADS)].rearrange("p (k c) -> p k c", k=2)
            for b in range(2):
                for k in range(KT):
                    m = mm([IA, IB][b][0:HEADS, :], wsh[:, k, P:P + HEADS], xT[:, k, b * SEQ:(b + 1) * SEQ],
                           start=k == 0, stop=k == 1)
                m.then_inc(pro_p, 1)
            wr = F[:, 1, 0:2 * (EXPERTS + 1)].rearrange("p (k c) -> p k c", k=2)
            for q in range(2):
                for t in range(4):
                    for k in range(KT):
                        m = mm(LV[q][:, t * 80:t * 80 + EXPERTS + 1],
                               xT[:, k, (4 * q + t) * P:(4 * q + t + 1) * P], wr[:, k, :],
                               start=k == 0, stop=k == 1)
                m.then_inc(pro_p, 1)
            pe.wait_ge(pro_a, PA_FAGA)
            for b in range(2):
                for g in range(2):
                    for k in range(KT):
                        m = mm((FB + [OX])[2 * b + g][0:INNER, :], wsh[:, k, g * INNER:(g + 1) * INNER],
                               xT[:, k, b * SEQ:(b + 1) * SEQ], start=k == 0, stop=k == 1)
                m.then_inc(pro_p, 1)
            for j in range(4):
                if j == 0:
                    pe.wait_ge(pro_v, PV_SH)
                    pe.wait_ge(pro_a, PA_BETA)
                if j >= 2:
                    pe.wait_ge(pro_v, 33 + j - 2)
                for t in range(2):
                    tk = 2 * j + t
                    m = mm([IA, IB][j % 2][:, t * HID:(t + 1) * HID],
                           sh_h(tk), F[0:INNER, 3, 0:HID],
                           start=True, stop=True)
                m.then_inc(pro_p, 1)
            pe.wait_ge(pro_v, PV_ROUTE)
            pe.wait_ge(pro_a, PA_SGATE)
            for q in range(2):
                for t in range(4):
                    m = pe.transpose(LV[q][0:EXPERTS, t * P:(t + 1) * P], route_tok(4 * q + t), ident[:, :])
                m.then_inc(pro_p, 1)

            def proj(v, b, which, bank, ready):
                for k in range(KT):
                    m = mm(bank[:, :], wp[:, 2 * which + k, :], xT[:, k, b * SEQ:(b + 1) * SEQ],
                           start=k == 0, stop=k == KT - 1)
                m.then_inc(ready, 1)

            def prep_decay(v, b, vh):
                pe.wait_ge(d_wp, vh * 16 + 16)
                after(pe, v_f, v - 2)
                mm(FB[0][:, :], wp[:, 6, :], fa[:, b * SEQ:(b + 1) * SEQ], start=True, stop=True).then_inc(m_g, 1)
                mm(FB[1][:, :], wp[:, 7, :], ga[:, b * SEQ:(b + 1) * SEQ], start=True, stop=True).then_inc(m_go, 1)

            def prep_q(v, b):
                proj(v, b, 0, FB[2], m_q)

            def prep_k(v, b):
                after(pe, a_abs, v)
                proj(v, b, 1, FB[0], m_k)

            def prep_v(v, b):
                after(pe, a_gate, v)
                proj(v, b, 2, FB[1], m_v)

            def prep_norm(v, n):
                after(pe, p_sq[n], v)
                after(pe, v_conv[n], v)
                mm(FB[2 if n == 0 else 0][:, :], ones[:, :], sq[n][:, :], start=True, stop=True)\
                    .then_inc([m_nq, m_nk][n], 1)

            def level(u, n):
                if n == 0:
                    after(pe, v_norm[1], u)
                    after(pe, v_norm[0], u)
                    after(pe, v_sacc, u - 1)
                if n >= 2:
                    after(pe, v_lv, u, n - 1)
                if n:
                    after(pe, v_prod, u, n)
                out4 = LV[n % 2][:, :].rearrange("p (w c i) -> p w c i", w=2, c=NC)
                for c in range(NC):
                    if n == 0:
                        m = mm(LV[0][:, c * CH:(c + 1) * CH], kn[:, c * CH:(c + 1) * CH],
                               qn[:, c * CH:(c + 1) * CH], start=True, stop=True)
                    else:
                        m = mm(out4[:, :, c, :], KL[:, n - 1, c * CH:(c + 1) * CH],
                               KQL[:, n - 1, :, c * (CH // 2):(c + 1) * (CH // 2)], start=True, stop=True)
                m.then_inc(m_lv, 1)

            def turn(u):
                after(pe, p_vb, u)
                after(pe, a_orn, u - 1)
                for c in range(NC):
                    m = pe.transpose(OX[:, c * P:(c + 1) * P], vb[:, c * CH:(c + 1) * CH], ident[:, :])
                m.then_inc(m_tr, 1)
                after(pe, v_full, u)
                for c in range(NC):
                    m = pe.transpose(IA[:, c * P:(c + 1) * P], kS[:, c * CH:(c + 1) * CH], ident[:, :])
                m.then_inc(m_tr, 1)

            def turn_first(u):
                after(pe, v_og, u - 1)
                after(pe, v_lv, u, 2)
                for c in range(NC):
                    m = pe.transpose(IB[:, c * P:(c + 1) * P], Bt[:, 0, c * CH:(c + 1) * CH], ident[:, :])
                m.then_inc(m_tr, 1)

            def inv_w(u, l):
                after(pe, v_lv, u, l + 2)
                if l == 1:
                    after(pe, a_tr, u)
                for h in range(2):
                    after(pe, v_t, u, 2 * l - 1 + h)
                    for c in range(2 * h, 2 * h + 2):
                        m = mm([IA, IB][h][:, (c % 2) * P:(c % 2 + 1) * P], Bt[:, l, c * CH:(c + 1) * CH], T[:, c, :],
                               start=True, stop=True)
                    m.then_inc(m_w, 1)

            def inv_t(u, l):
                for h in range(2):
                    after(pe, a_w, u, 2 * (l - 1) + h + 1)
                    for c in range(2 * h, 2 * h + 2):
                        m = mm([IA, IB][h][:, (c % 2) * P:(c % 2 + 1) * P], W[:, c, :], Tt[:, c, :],
                               start=True, stop=True)
                        if l < LEV - 1:
                            m = mm([IA, IB][h][:, (2 + c % 2) * P:(3 + c % 2) * P], Tt[:, c, :], W[:, c, :],
                                   start=True, stop=True)
                    m.then_inc(m_t, 1)

            def chain_r(u, c):
                after(pe, v_s, u, c)
                mm(IA[:, 0:P], kbG[:, c * CH:(c + 1) * CH], S[:, c % 2, :], start=True, stop=True).then_inc(m_r, 1)

            def chain_u(u, c):
                if c == 0:
                    after(pe, v_t, u)
                    rhs = vbT[:, 0, :]
                else:
                    after(pe, v_r, u, c)
                    rhs = R[:, c % 2, :]
                mm(IA[:, P:2 * P], Tt[:, c, :], rhs, start=True, stop=True).then_inc(m_u, 1)

            def chain_so(u, c):
                after(pe, a_u, u, c + 1)
                if c < NC - 1:
                    mm(IA[:, 2 * P:3 * P], kStok[:, c, :], U[:, c % 2, :], start=True, stop=True).then_inc(m_s, 1)
                if c:
                    mm(IB[:, c * CH:(c + 1) * CH], S[:, c % 2, :], qG[:, c * CH:(c + 1) * CH],
                       start=True, stop=False)
                mm(IB[:, c * CH:(c + 1) * CH], U[:, c % 2, :], Pt[:, c * CH:(c + 1) * CH],
                   start=c == 0, stop=True).then_inc(m_o, 1)

            def gate_up(u, t, g, nxt):
                if t == 0 and g == 0:
                    pe.wait_ge(d_gu, u * 16 + 16)
                    if nxt:
                        after(pe, v_conv[2], u + 1)
                    else:
                        after(pe, v_f, u - 1)
                elif not nxt and not (t and g):
                    pass
                elif t == 0:
                    after(pe, a_nln[0], u + 1)
                elif g == 0:
                    after(pe, a_nln[1], u + 1)
                else:
                    after(pe, a_sg, u, 1)
                for k in range(KT):
                    m = mm(FB[(1 + 2 * t + g) % 3][:, :], gu[:, k, g, :], xT[:, k, t * SEQ:(t + 1) * SEQ],
                           start=k == 0, stop=k == KT - 1)
                m.then_inc([m_gate, m_up][g], 1)

            def down(u, j):
                if j == 0:
                    pe.wait_ge(d_dw, u * 16 + 16)
                    after(pe, v_h, u, 1)
                elif j == 1:
                    after(pe, a_sg, u, 2)
                elif j == 2:
                    after(pe, v_h, u, 2)
                else:
                    after(pe, v_f, u, 1)
                after(pe, p_h, u, j // 2 + 1)
                for t in range(2):
                    c = (2 * j + t) % 4
                    m = mm(FB[(2 + j) % 3][:, t * HID:(t + 1) * HID], hw[:, j // 2, c * P:(c + 1) * P], dw[:, :],
                           start=True, stop=True)
                m.then_inc(m_down, 1)

            def norm_out(u):
                after(pe, a_osq, u)
                mm(OX[:, :], ones[:, :], osq[:, :], start=True, stop=True).then_inc(m_ss, 1)

            def project_out(u, b, head):
                if b == 0:
                    pe.wait_ge(d_wo, head * 16 + 16)
                after(pe, v_osc, u)
                after(pe, v_lv, u)
                for j in range(2):
                    for t in range(2):
                        c = 2 * j + t
                        m = mm(LV[j][:, t * HID:(t + 1) * HID], osc[:, c * CH:(c + 1) * CH], wo[:, :],
                               start=True, stop=True)
                    m.then_inc(m_wo, 1)

            def unit(u, b, head, nxt, nxt_head):
                level(u, 0)
                level(u, 1)
                turn(u)
                if nxt:
                    prep_decay(u + 1, 1 - b, nxt_head)
                turn_first(u)
                level(u, 2)
                for l in range(1, LEV):
                    inv_w(u, l)
                    if l < LEV - 1:
                        level(u, l + 2)
                    if nxt:
                        if l == 1:
                            prep_q(u + 1, 1 - b)
                        if l == 2:
                            prep_k(u + 1, 1 - b)
                        if l == 3:
                            prep_v(u + 1, 1 - b)
                        if l == 5:
                            prep_norm(u + 1, 0)
                        if l == 6:
                            prep_norm(u + 1, 1)
                    inv_t(u, l)
                chain_u(u, 0)
                gate_up(u, 0, 0, nxt)
                gate_up(u, 0, 1, nxt)
                chain_so(u, 0)
                chain_r(u, 1)
                gate_up(u, 1, 0, nxt)
                chain_u(u, 1)
                chain_so(u, 1)
                chain_r(u, 2)
                gate_up(u, 1, 1, nxt)
                chain_u(u, 2)
                chain_so(u, 2)
                chain_r(u, 3)
                down(u, 0)
                chain_u(u, 3)
                down(u, 1)
                chain_so(u, 3)
                down(u, 2)
                norm_out(u)
                down(u, 3)
                project_out(u, b, head)

            pe.wait_ge(pro_v, PV_END)
            pe.wait_ge(pro_a, PA_ROUTE)
            prep_decay(0, 0, 0)
            prep_q(0, 0)
            prep_k(0, 0)
            prep_v(0, 0)
            prep_norm(0, 0)
            prep_norm(0, 1)
            unit(0, 0, 0, True, 0)
            unit(1, 1, 0, True, 1)
            with pe.Fori(1, HEADS - 1) as h:
                unit(2 * h, 0, h, True, h)
                unit(2 * h + 1, 1, h, True, h + 1)
            unit(UNITS - 2, 0, HEADS - 1, True, HEADS - 1)
            unit(UNITS - 1, 1, HEADS - 1, False, 0)

        @block.vector
        def _(ve):
            stt, ts, tt = ve.scalar_tensor_tensor, ve.tensor_scalar, ve.tensor_tensor

            def chained(ins, n):
                ins.then_inc(pro_v, 1)
                ve.wait_ge(pro_v, n)

            ve.wait_ge(d_x, 16)
            X = s_acc[:, :, :]
            chained(ve.tensor_reduce(mean, X, AX_X, ALU.add), 1)
            chained(ts(mean, mean, 1.0 / HID, None, ALU.mult), 2)
            chained(tt(s_acc[:, :, :], X, mean.unsqueeze(2).to_broadcast([P, TT, HID]), ALU.subtract), 3)
            chained(tt(f_acc[:, :, :], X, X, ALU.mult), 4)
            chained(ve.tensor_reduce(var, f_acc[:, :, :], AX_X, ALU.add), 5)
            ve.wait_ge(pro_a, PA_RSTD)
            chained(tt(f_acc[:, :, :], X, rstd.unsqueeze(2).to_broadcast([P, TT, HID]), ALU.mult), 6)
            for b in range(2):
                ve.wait_ge(pro_p, 12 + b + 1)
                ve.wait_ge(pro_a, PA_BETA + b + 1)
                tt(sh_hidden[0:INNER, b * SEQ:(b + 1) * SEQ], sh_silu[0:INNER, b * SEQ:(b + 1) * SEQ],
                   (FB + [OX])[2 * b + 1][0:INNER, :], ALU.mult).then_inc(pro_v, 1)
            for q in range(2):
                ve.wait_ge(pro_p, 10 + q + 1)
                ve.tensor_copy(logits[:, 4 * q:4 * q + 4, :],
                               LV[q][:, 0:320].rearrange("p (t e) -> p t e", e=80)[:, :, 0:EXPERTS]).then_inc(pro_v, 1)
            ve.wait_ge(pro_v, 10)
            for t in range(TT):
                ve.max(top8[:, t, :], logits[:, t, :]).then_inc(pro_v, 1)
            ve.wait_ge(pro_v, 18)
            for t in range(TT):
                ve.match_replace(lmask[:, t, :], top8[:, t, :], logits[:, t, :], NEG_BIG).then_inc(pro_v, 1)
            ve.wait_ge(pro_v, 26)
            chained(tt(lmask[:, :, :], lmask[:, :, :], logits[:, :, :], ALU.not_equal), 27)
            chained(tt(logits[:, :, :], logits[:, :, :], top8[:, :, 0:1].to_broadcast([P, TT, EXPERTS]),
                       ALU.subtract), 28)
            ve.wait_ge(pro_a, PA_EXPR)
            chained(tt(routed[:, :, :], lmask[:, :, :], logits[:, :, :], ALU.mult), 29)
            chained(ve.tensor_reduce(rsum, routed[:, :, :], AX_X, ALU.add), 30)
            chained(ve.reciprocal(rsum, rsum), 31)
            chained(tt(routed[:, :, :], routed[:, :, :], rsum.unsqueeze(2).to_broadcast([P, TT, EXPERTS]),
                       ALU.mult), 32)
            ve.wait_ge(pro_a, PA_SGATE)
            for j in range(4):
                ve.wait_ge(pro_p, 14 + j + 1)
                tt(f_acc[:, 2 * j:2 * j + 2, :], [IA, IB][j % 2][:, :].rearrange("p (t h) -> p t h", t=2),
                   shg[:, 2 * j:2 * j + 2].unsqueeze(2).to_broadcast([P, 2, HID]), ALU.mult).then_inc(pro_v, 1)
            ve.wait_ge(pro_a, PA_ROUTE)
            ve.wait_ge(pro_p, 20)
            ve.memset(s_acc[:, :, :], 0.0).then_inc(pro_v, 1)
            ve.memset(zero[:, :], 0.0)
            ve.memset(Bt[:, :, :], 0.0).then_inc(pro_v, 1)
            ve.wait_ge(pro_v, 38)

            def softplus_series(v):
                after(ve, a_e, v)
                ts(hz[:, :], ez[:, :], -0.25, None, ALU.mult).then_inc(v_sp, 1)
                for n, c in enumerate((1.0 / 3, -0.5, 1.0)):
                    after(ve, v_sp, v, n + 1)
                    stt(hz[:, :], hz[:, :], c, ez[:, :], ALU.add, ALU.mult).then_inc(v_sp, 1)
                after(ve, a_ln, v)
                ts(small[:, :], ez[:, :], SMALL, None, ALU.is_lt).then_inc(v_sp, 1)

            def conv(v, n, j):
                if j == 1:
                    after(ve, a_tap[n], v)
                else:
                    after(ve, v_conv[n], v, j - 1)
                stt(raw[n][:, j:SEQ], [FB[2], FB[0], FB[1]][n][:, 0:SEQ - j],
                    taps[:, n, TAPS - 1 - j:TAPS - j], raw[n][:, j:SEQ], ALU.mult, ALU.add)\
                    .then_inc(v_conv[n], 1)

            def softplus_rest(v):
                ve.copy_predicated(lz[:, :], small[:, :], hz[:, :]).then_inc(v_sp, 1)
                after(ve, v_sp, v, 6)
                after(ve, a_abs, v)
                tt(lz[:, :], lz[:, :], relz[:, :], ALU.add).then_inc(v_sp, 1)
                after(ve, v_sp, v, 7)
                after(ve, a_full, v - 1)
                after(ve, p_sum, v - 1)
                ts(pre[:, :], lz[:, :], exp_a[:, :], -1.0, ALU.mult, ALU.mult).then_inc(v_sp, 1)

            def normalise(v, n):
                after(ve, a_rn[n], v)
                tt([qn, kn][n][:, :], act[n][:, :], rn[n][:, :], ALU.mult).then_inc(v_norm[n], 1)

            def product(v, l):
                s = 1 << l
                if l == 0:
                    after(ve, v_norm[0], v)
                    after(ve, v_norm[1], v)
                    after(ve, p_kb, v)
                after(ve, a_F, v, l + 1)
                tt(KL[:, l, :], kn[:, :], F[:, l, :], ALU.mult)
                for w, src in enumerate((kb, qn)):
                    m = tt(KQL[:, l, w, :].rearrange("p (n s) -> p n s", s=s), halves(src[:, :], s)[:, :, 1, :],
                           halves(F[:, l, :], s)[:, :, 1, :], ALU.mult)
                m.then_inc(v_prod, 1)

            def full_products(v, b):
                after(ve, a_full, v)
                after(ve, m_o, v - 1)
                after(ve, m_tr, v - 1, 2)
                tt(kbG[:, :], kb[:, :], Fpre[:, :], ALU.mult)
                tt(qG[:, :], qn[:, :], Fpre[:, :], ALU.mult)
                ve.tensor_copy(dec[:, b, :], c4(Fpre[:, :])[:, :, CH - 1])
                tt(kS[:, :], kn[:, :], Fsuf[:, :], ALU.mult).then_inc(v_full, 1)

            def level(u, n):
                after(ve, m_lv, u, n + 1)
                if n == 0:
                    tt(c4(Pt[:, :]), c4(LV[0][:, :]), ident4[:, :, :], ALU.mult).then_inc(v_lv, 1)
                    return
                after(ve, v_lv, u, n)
                l, bank = n - 1, LV[n % 2]
                s = 1 << l
                split = lambda ap: ap.rearrange("p (n s) -> p n s", s=s)
                tt(halves(Bt[:, l, :], s)[:, :, 1, :], split(bank[:, 0:HALF]), split(mask[:, l, :]), ALU.mult)
                ve.copy_predicated(halves(Pt[:, :], s)[:, :, 1, :], split(mask[:, l, :].bitcast(U32)),
                                   split(bank[:, HALF:SEQ])).then_inc(v_lv, 1)

            def first_inverse(u):
                after(ve, m_tr, u, 3)
                after(ve, v_lv, u, 2)
                for h in range(2):
                    c = slice(2 * h, 2 * h + 2)
                    tt(T[:, c, :], ident4[:, c, :], c4(IB[:, :])[:, c, :], ALU.subtract)
                    tt(Tt[:, c, :], ident4[:, c, :], c4(Bt[:, 0, :])[:, c, :], ALU.subtract).then_inc(v_t, 1)

            def inverse(u, l):
                for h in range(2):
                    c = slice(2 * h, 2 * h + 2)
                    after(ve, m_t, u, 2 * (l - 1) + h + 1)
                    after(ve, v_t, u, 2 * (l - 1) + h + 1)
                    if l < LEV - 1:
                        tt(T[:, c, :], T[:, c, :], c4([IA, IB][h][:, :])[:, 2:4, :], ALU.subtract)
                    tt(Tt[:, c, :], Tt[:, c, :], c4([IA, IB][h][:, :])[:, 0:2, :], ALU.subtract).then_inc(v_t, 1)

            def right_side(u, c):
                after(ve, m_r, u, c)
                after(ve, a_tr, u, 1)
                tt(R[:, c % 2, :], vbT[:, c, :], IA[:, 0:P], ALU.subtract).then_inc(v_r, 1)

            def state(u, b, c):
                after(ve, m_s, u, c + 1)
                if c == 0:
                    ve.tensor_copy(S[:, 1, :], IA[:, 2 * P:3 * P]).then_inc(v_s, 1)
                    return
                after(ve, v_s, u, c)
                stt(S[:, (c + 1) % 2, :], S[:, c % 2, :], dec[:, b, c:c + 1], IA[:, 2 * P:3 * P],
                    ALU.mult, ALU.add).then_inc(v_s, 1)

            def hidden(u, t):
                after(ve, a_sg, u, t + 1)
                after(ve, m_up, u, t + 1)
                after(ve, p_h, u - 1)
                tt(hh[:, t, :], sg[:, t, :], FB[(2 + 2 * t) % 3][:, :], ALU.mult).then_inc(v_h, 1)

            def add_down(u, j):
                after(ve, m_down, u, j + 1)
                f = f_acc[:, 2 * j:2 * j + 2, :].rearrange("p t h -> p (t h)")
                tt(f, f, FB[(2 + j) % 3][:, :], ALU.add).then_inc(v_f, 1)

            def output(u, b):
                after(ve, a_osq, u)
                after(ve, a_gate, u)
                stt(ogw[:, :], IB[:, :], onorm[:, :], gate[:, b, :], ALU.mult, ALU.mult).then_inc(v_og, 1)
                after(ve, a_orn, u)
                after(ve, v_og, u)
                tt(osc[:, :], ogw[:, :], orn[:, :], ALU.mult).then_inc(v_osc, 1)

            def add_out(u, b):
                for j in range(2):
                    after(ve, m_wo, u, j + 1)
                    t = 4 * b + 2 * j
                    a = s_acc[:, t:t + 2, :].rearrange("p t h -> p (t h)")
                    tt(a, a, LV[j][:, :], ALU.add).then_inc(v_sacc, 1)

            def unit(u, b, nxt):
                v, vb_ = u + 1, 1 - b
                level(u, 0)
                level(u, 1)
                first_inverse(u)
                level(u, 2)
                for l in range(1, LEV):
                    if l < LEV - 1:
                        level(u, l + 2)
                    if nxt:
                        if l == 1:
                            softplus_series(v)
                        if l == 2:
                            after(ve, v_sp, v, 5)
                            conv(v, 0, 1)
                            softplus_rest(v)
                            conv(v, 0, 2)
                            conv(v, 0, 3)
                        if l == 3:
                            for j in (1, 2, 3):
                                conv(v, 1, j)
                        if l == 4:
                            for j in (1, 2, 3):
                                conv(v, 2, j)
                    inverse(u, l)
                if nxt:
                    normalise(v, 0)
                    normalise(v, 1)
                state(u, b, 0)
                if nxt:
                    product(v, 0)
                right_side(u, 1)
                state(u, b, 1)
                hidden(u, 0)
                if nxt:
                    product(v, 1)
                    product(v, 2)
                right_side(u, 2)
                state(u, b, 2)
                hidden(u, 1)
                if nxt:
                    product(v, 3)
                right_side(u, 3)
                if nxt:
                    product(v, 4)
                add_down(u, 0)
                add_down(u, 1)
                if nxt:
                    product(v, 5)
                    product(v, 6)
                add_down(u, 2)
                output(u, b)
                add_down(u, 3)
                if nxt:
                    full_products(v, vb_)
                add_out(u, b)

            softplus_series(0)
            after(ve, v_sp, 0, 5)
            conv(0, 0, 1)
            softplus_rest(0)
            for n, j in ((0, 2), (0, 3), (1, 1), (1, 2), (1, 3), (2, 1), (2, 2), (2, 3)):
                conv(0, n, j)
            normalise(0, 0)
            normalise(0, 1)
            for l in range(LEV):
                product(0, l)
            full_products(0, 0)
            unit(0, 0, True)
            unit(1, 1, True)
            with ve.Fori(1, HEADS - 1) as h:
                unit(2 * h, 0, True)
                unit(2 * h + 1, 1, True)
            unit(UNITS - 2, 0, True)
            unit(UNITS - 1, 1, False)
            ve.wait_ge(d_x, 32)
            xr = KL[:, 0:4, :].rearrange("p a b -> p (a b)").rearrange("p (t h) -> p t h", t=TT)
            after(ve, v_sacc, UNITS - 1)
            for t in range(4):
                c = slice(2 * t, 2 * t + 2)
                ve.wait_ge(end_a, t + 1)
                tt(s_acc[:, c, :], s_acc[:, c, :], f_acc[:, c, :], ALU.mult).then_inc(end_v, 1)
                ve.wait_ge(end_v, 2 * t + 1)
                tt(s_acc[:, c, :], s_acc[:, c, :], xr[:, c, :], ALU.add).then_inc(end_v, 1)

        @block.scalar
        def _(ac):
            A = ac.activation
            eps, lscale, ln_eps, one = [biases[:, n:n + 1] for n in range(4)]

            ac.wait_ge(d_const, NCONST)
            ac.wait_ge(pro_v, PV_VAR)
            A(var, var, ACT.Ln, bias=ln_eps, scale=1.0 / HID).then_inc(pro_a, 1)
            ac.wait_ge(pro_a, 1)
            A(rstd, var, ACT.Exp, scale=-0.5).then_inc(pro_a, 1)
            for q in range(4):
                ac.wait_ge(pro_p, q + 1)
                A(xT[:, :, 2 * q * P:(2 * q + 2) * P], (LV + [IA, IB])[q][:, :].rearrange("p (k t) -> p k t", k=KT),
                  ACT.Copy).then_inc(pro_a, 1)
            for n in range(4):
                ac.wait_ge(pro_p, 5 + n)
                A([fa, ga][n // 2][:, (n % 2) * SEQ:(n % 2 + 1) * SEQ], (FB + [OX])[n][:, :], ACT.Copy).then_inc(pro_a, 1)
            for b in range(2):
                ac.wait_ge(pro_p, 9 + b)
                A(KL[0:HEADS, 2 + b, :], [IA, IB][b][0:HEADS, :], ACT.Sigmoid).then_inc(pro_a, 1)
            for b in range(2):
                ac.wait_ge(pro_p, 13 + b)
                A(sh_silu[0:INNER, b * SEQ:(b + 1) * SEQ], (FB + [OX])[2 * b][0:INNER, :], ACT.Silu).then_inc(pro_a, 1)
            ac.wait_ge(pro_v, 10)
            for q in range(2):
                A(shg[:, 4 * q:4 * q + 4], LV[q][:, 0:320].rearrange("p (t e) -> p t e", e=80)[:, :, EXPERTS],
                  ACT.Sigmoid).then_inc(pro_a, 1)
            ac.wait_ge(pro_v, 28)
            A(logits[:, :, :], logits[:, :, :], ACT.Exp).then_inc(pro_a, 1)
            for q in range(2):
                ac.wait_ge(pro_p, 19 + q)
                A(KL[0:EXPERTS, q, :], LV[q][0:EXPERTS, :], ACT.Copy).then_inc(pro_a, 1)

            def decay_in(v, vh):
                ac.wait_ge(d_wp, vh * 16 + 16)
                after(ac, m_g, v)
                after(ac, v_sp, v - 1)
                A(absz[:, :], FB[0][:, :], ACT.Abs, bias=dtb).then_inc(a_abs, 1)
                A(relz[:, :], FB[0][:, :], ACT.Relu, bias=dtb).then_inc(a_abs, 1)
                after(ac, a_abs, v, 1)
                A(ez[:, :], absz[:, :], ACT.Exp, scale=-1.0).then_inc(a_e, 1)
                A(exp_a[:, :], a_log, ACT.Exp)
                after(ac, a_e, v)
                A(lz[:, :], ez[:, :], ACT.Ln, bias=one).then_inc(a_ln, 1)

            def gate_in(v, vb_):
                after(ac, m_go, v)
                after(ac, v_og, v - 2)
                A(gate[:, vb_, :], FB[1][:, :], ACT.Sigmoid).then_inc(a_gate, 1)

            def tap(v, n):
                after(ac, [m_q, m_k, m_v][n], v)
                A(raw[n][:, :], [FB[2], FB[0], FB[1]][n][:, :], ACT.Copy, scale=taps[:, n, TAPS - 1:TAPS])\
                    .then_inc(a_tap[n], 1)

            def silu(v, n):
                after(ac, v_conv[n], v)
                if n == 2:
                    after(ac, p_vb, v - 1)
                else:
                    after(ac, p_sq[n], v - 1)
                    after(ac, v_norm[n], v - 1)
                A(act[n][:, :], raw[n][:, :], ACT.Silu).then_inc(a_silu[n], 1)

            def inv_norm(v, n):
                after(ac, [m_nq, m_nk][n], v)
                after(ac, v_norm[n], v - 1)
                A(rn[n][:, :], FB[2 if n == 0 else 0][:, :], ACT.Ln, bias=eps).then_inc(a_nln[n], 1)
                after(ac, a_nln[n], v)
                if n == 0:
                    A(rn[n][:, :], rn[n][:, :], ACT.Exp, scale=-0.5, bias=lscale).then_inc(a_rn[n], 1)
                else:
                    A(rn[n][:, :], rn[n][:, :], ACT.Exp, scale=-0.5).then_inc(a_rn[n], 1)

            def decay(v, l):
                s = 1 << l
                if l == 0:
                    after(ac, v_sp, v)
                    after(ac, p_zero, v)
                else:
                    after(ac, p_sum, v, 2 * l)
                after(ac, v_prod, v - 1, l + 1)
                A(halves(F[:, l, :], s)[:, :, 0, :], halves(suf[:, :], s)[:, :, 0, :], ACT.Exp)
                A(halves(F[:, l, :], s)[:, :, 1, :], halves(pre[:, :], s)[:, :, 1, :], ACT.Exp).then_inc(a_F, 1)

            def full_decay(v):
                after(ac, p_sum, v)
                after(ac, v_full, v - 1)
                A(Fpre[:, :], pre[:, :], ACT.Exp)
                A(Fsuf[:, :], suf[:, :], ACT.Exp).then_inc(a_full, 1)

            def copy_turned(u):
                after(ac, m_tr, u, 1)
                after(ac, v_r, u - 1)
                A(vbT[:, :, :], c4(OX[:, :]), ACT.Copy).then_inc(a_tr, 1)
                after(ac, m_tr, u, 2)
                A(kStok[:, :, :], c4(IA[:, :]), ACT.Copy).then_inc(a_tr, 1)

            def copy_w(u, l):
                for h in range(2):
                    after(ac, m_w, u, 2 * (l - 1) + h + 1)
                    A(W[:, 2 * h:2 * h + 2, :], c4([IA, IB][h][:, :])[:, 0:2, :], ACT.Copy).then_inc(a_w, 1)

            def copy_u(u, c):
                after(ac, m_u, u, c + 1)
                A(U[:, c % 2, :], IA[:, P:2 * P], ACT.Copy).then_inc(a_u, 1)

            def silu_gate(u, t):
                after(ac, m_gate, u, t + 1)
                after(ac, v_h, u - 1)
                A(sg[:, t, :], FB[(1 + 2 * t) % 3][:, :], ACT.Silu).then_inc(a_sg, 1)

            def out_norm(u):
                after(ac, m_o, u)
                A(osq[:, :], IB[:, :], ACT.Square).then_inc(a_osq, 1)
                after(ac, m_ss, u)
                after(ac, v_osc, u - 1)
                A(orn[:, :], OX[:, :], ACT.Ln, scale=1.0 / D, bias=eps).then_inc(a_oln, 1)
                after(ac, a_oln, u)
                A(orn[:, :], orn[:, :], ACT.Exp, scale=-0.5).then_inc(a_orn, 1)

            def unit(u, b, nxt, nxt_head):
                v, vb_ = u + 1, 1 - b
                copy_turned(u)
                if nxt:
                    decay_in(v, nxt_head)
                copy_w(u, 1)
                if nxt:
                    gate_in(v, vb_)
                    tap(v, 0)
                copy_w(u, 2)
                if nxt:
                    tap(v, 1)
                    silu(v, 0)
                copy_w(u, 3)
                if nxt:
                    tap(v, 2)
                    silu(v, 1)
                copy_w(u, 4)
                if nxt:
                    silu(v, 2)
                copy_w(u, 5)
                if nxt:
                    decay(v, 0)
                copy_w(u, 6)
                if nxt:
                    inv_norm(v, 0)
                    inv_norm(v, 1)
                    decay(v, 1)
                copy_u(u, 0)
                if nxt:
                    decay(v, 2)
                silu_gate(u, 0)
                silu_gate(u, 1)
                copy_u(u, 1)
                if nxt:
                    decay(v, 3)
                copy_u(u, 2)
                if nxt:
                    decay(v, 4)
                copy_u(u, 3)
                if nxt:
                    decay(v, 5)
                    decay(v, 6)
                out_norm(u)
                if nxt:
                    full_decay(v)

            decay_in(0, 0)
            gate_in(0, 0)
            for n in range(3):
                tap(0, n)
            for n in range(3):
                silu(0, n)
            inv_norm(0, 0)
            inv_norm(0, 1)
            for l in range(LEV):
                decay(0, l)
            full_decay(0)
            unit(0, 0, True, 0)
            unit(1, 1, True, 1)
            with ac.Fori(1, HEADS - 1) as h:
                unit(2 * h, 0, True, h)
                unit(2 * h + 1, 1, True, h + 1)
            unit(UNITS - 2, 0, True, HEADS - 1)
            unit(UNITS - 1, 1, False, 0)
            after(ac, v_f, UNITS - 1)
            for t in range(4):
                c = slice(2 * t, 2 * t + 2)
                A(f_acc[:, c, :], f_acc[:, c, :], ACT.Silu).then_inc(end_a, 1)

        @block.gpsimd
        def _(gp):
            tt = gp.tensor_tensor

            def start_sums(v):
                after(gp, a_full, v - 1)
                tt(suf[:, :], zero[:, :], zero[:, :], ALU.add).then_inc(p_zero, 1)

            def merge(v, l):
                s = 1 << l
                after(gp, a_F, v, l + 1)
                after(gp, p_sum, v, 2 * l)
                if l == 0:
                    after(gp, p_zero, v)
                    after(gp, v_sp, v)
                sv, pv = halves(suf[:, :], s), halves(pre[:, :], s)
                n = SEQ // (2 * s)
                last = pv[:, :, :, s - 1:s]
                tt(sv[:, :, 0, :], sv[:, :, 0, :], last[:, :, 1, :].to_broadcast([P, n, s]), ALU.add).then_inc(p_sum, 1)
                after(gp, p_sum, v, 2 * l + 1)
                tt(pv[:, :, 1, :], pv[:, :, 1, :], last[:, :, 0, :].to_broadcast([P, n, s]), ALU.add).then_inc(p_sum, 1)

            def square(v, n):
                after(gp, a_silu[n], v)
                after(gp, [m_nq, m_nk][n], v - 1)
                tt(sq[n][:, :], act[n][:, :], act[n][:, :], ALU.mult).then_inc(p_sq[n], 1)

            def beta(v):
                gp.wait_ge(d_bb, v * 16 + 16)
                after(gp, a_silu[2], v)
                after(gp, m_tr, v - 1, 1)
                tt(vb[:, :], act[2][:, :], bb[:, :], ALU.mult).then_inc(p_vb, 1)
                after(gp, v_norm[1], v)
                after(gp, v_full, v - 1)
                tt(kb[:, :], kn[:, :], bb[:, :], ALU.mult).then_inc(p_kb, 1)

            def weigh(u, t):
                gp.wait_ge(d_wbc, u * 32 + 32)
                after(gp, v_h, u, t + 1)
                after(gp, m_down, u - 1)
                tt(hw[:, t, :], hh[:, t, :], wbc[:, t * SEQ:(t + 1) * SEQ], ALU.mult).then_inc(p_h, 1)

            def unit(u, nxt):
                v = u + 1
                if nxt:
                    start_sums(v)
                    square(v, 0)
                    square(v, 1)
                    merge(v, 0)
                    beta(v)
                    merge(v, 1)
                    merge(v, 2)
                weigh(u, 0)
                if nxt:
                    merge(v, 3)
                weigh(u, 1)
                if nxt:
                    merge(v, 4)
                    merge(v, 5)
                    merge(v, 6)

            gp.wait_ge(pro_v, PV_END)
            start_sums(0)
            square(0, 0)
            square(0, 1)
            beta(0)
            for l in range(LEV):
                merge(0, l)
            unit(0, True)
            unit(1, True)
            with gp.Fori(1, HEADS - 1) as h:
                unit(2 * h, True)
                unit(2 * h + 1, True)
            unit(UNITS - 2, True)
            unit(UNITS - 1, False)


def kernel(**inputs):
    import concourse.bacc as _bacc
    from concourse.bass_utils import run_bass_kernel_spmd as _run

    g = {k.replace("L0_attn_", "").replace("L0_ffn_", ""): np.ascontiguousarray(v) for k, v in inputs.items()}

    def k_tiles(w):
        return w.reshape(KT, P, -1).transpose(1, 0, 2)

    def per_head(w):
        return w.reshape(KT, P, HEADS, D).transpose(2, 1, 0, 3)

    def head_cols(w, n):
        return w.reshape(HEADS, D, n)

    heads = [per_head(g["Wq"]), per_head(g["Wk"]), per_head(g["Wv"]),
             g["Wfb"].reshape(P, HEADS, 1, D).transpose(1, 0, 2, 3), g["Wgb"].reshape(P, HEADS, 1, D).transpose(1, 0, 2, 3)]
    wproj = np.concatenate(
        [np.concatenate(heads, axis=2).reshape(HEADS, P, 8 * D), head_cols(g["conv_q_w"], TAPS),
         head_cols(g["conv_k_w"], TAPS), head_cols(g["conv_v_w"], TAPS), head_cols(g["dt_bias"], 1),
         np.broadcast_to(g["A_log"].reshape(HEADS, 1, 1), (HEADS, P, 1))], axis=2).reshape(HEADS * P, 8 * D + HC)
    guw = g["gu_w"].reshape(PAIRS, 2, 2, INNER, KT, P)
    consts = np.zeros((P, 3, P), np.float32)
    consts[:, 0] = np.eye(P, dtype=np.float32)
    consts[:, 1] = 1.0
    consts[:, 2, 0:4] = [NORM_EPS, -0.5 * np.log(D), LN_EPS, 1.0]
    masks = np.zeros((P, LEV, NC, CH // 2), np.float32)
    for l in range(LEV):
        s = 1 << l
        i = np.arange(CH).reshape(-1, 2, s)[:, 1].reshape(-1)
        j = np.arange(CH)[:, None]
        masks[:, l] = ((j // (2 * s) == i // (2 * s)) & (j % (2 * s) < s)).astype(np.float32)[:, None, :]
    arrays = {
        "x": g["hidden_states"].reshape(TOK, HID),
        "wproj": wproj,
        "wout": g["Wo"],
        "wab": k_tiles(np.concatenate([g["Wfa"], g["Wga"]], axis=1)),
        "wrouter": k_tiles(np.concatenate([g["gate_w"], g["sh_gate1_w"]], axis=0).T),
        "wshared": k_tiles(np.concatenate([g["sh_gate_w"].T, g["sh_up_w"].T, g["Wb"]], axis=1)),
        "wsh_down": g["sh_down_w"].T,
        "wgu": guw.transpose(0, 5, 4, 2, 1, 3).reshape(PAIRS * P, KT * 2 * P),
        "wdown": g["dp_w"].transpose(0, 2, 1).reshape(PAIRS * P, HID),
        "o_norm": g["o_norm_w"].reshape(P, 1),
        "consts": consts,
        "masks": masks.reshape(P, LEV, HALF),
    }
    arrays = {k: np.ascontiguousarray(v) for k, v in arrays.items()}
    nc = _bacc.Bacc("TRN2", target_bir_lowering=False, num_devices=1)
    aps = [nc.dram_tensor(k, v.shape, F32, kind="ExternalInput").ap() for k, v in arrays.items()]
    beta = nc.dram_tensor("beta_rows", [HEADS, TOK], F32, kind="Internal").ap()
    route = nc.dram_tensor("route_rows", [EXPERTS, TOK], F32, kind="Internal").ap()
    out = nc.dram_tensor("out", [TOK, HID], F32, kind="ExternalOutput").ap()
    build(nc, *aps, beta, route, out)
    r = _run(nc, [arrays], core_ids=[0])
    return r.results[0]["out"].reshape(BATCH, SEQ, HID)
```

```python
from contextlib import ExitStack

import numpy as np

import concourse.bass as bass
from concourse import mybir

F32 = mybir.dt.float32
U32 = mybir.dt.uint32
ACT = mybir.ActivationFunctionType
ALU = mybir.AluOpType
AX_X = mybir.AxisListType.X

P = 128
BATCH, SEQ, HID = 2, 512, 256
TOK = BATCH * SEQ
TT = TOK // P
HEADS, D = 16, 128
KT = HID // P
CH = 128
NC = SEQ // CH
LEV = 7
LRING = 4
HALF = SEQ // 2
TAPS = 4
HC = 3 * TAPS + 2
EXPERTS, INNER = 64, 64
PAIRS = EXPERTS // 2
UNITS = HEADS * BATCH
NORM_EPS, LN_EPS = 1e-6, 1e-5
SMALL = 2.0 ** -6
NEG_BIG = -3.0e38
assert PAIRS == HEADS * BATCH


def build(nc, x_in, wproj, wout, wab, wrouter, wshared, wsh_down, wgu, wdown, o_norm, consts,
          masks, beta_dram, route_dram, out):
    with ExitStack() as ctx:
        def sb(name, *shape, dt=F32):
            return ctx.enter_context(nc.sbuf_tensor(name, [shape[0], *shape[1:]], dt))

        def sem(name):
            return ctx.enter_context(nc.semaphore(name))

        xT = sb("xT", P, KT, TOK)
        fa = sb("fa", P, TOK)
        ga = sb("ga", P, TOK)
        s_acc = sb("s_acc", P, TT, HID)
        f_acc = sb("f_acc", P, TT, HID)
        ident = sb("ident", P, P)
        ident4 = sb("ident4", P, NC, P)
        ones = sb("ones", P, P)
        mask = sb("mask", P, LEV, HALF)
        onorm = sb("onorm", P, 1)
        biases = sb("biases", P, 4)
        wpc = sb("wpc", P, 8 * P + HC)
        wp = wpc[:, 0:8 * P].rearrange("p (n c) -> p n c", c=P)
        taps = wpc[:, 8 * P:8 * P + 3 * TAPS].rearrange("p (n j) -> p n j", j=TAPS)
        dtb = wpc[:, 8 * P + 3 * TAPS:8 * P + 3 * TAPS + 1]
        a_log = wpc[:, 8 * P + 3 * TAPS + 1:8 * P + HC]
        exp_a = sb("exp_a", P, 1)
        wo = sb("wo", P, HID)
        gu = sb("gu", P, KT, 2, P)
        dw = sb("dw", P, HID)
        wbc = sb("wbc", P, TOK)
        bb = sb("bb", P, SEQ)
        KL = sb("KL", P, LRING, SEQ)
        KQL = sb("KQL", P, LRING, 2, HALF)
        kn = sb("kn", P, SEQ)
        qn = sb("qn", P, SEQ)
        kb = sb("kb", P, SEQ)
        vb = sb("vb", P, SEQ)
        kbG = sb("kbG", P, 2, SEQ)
        qG = sb("qG", P, 2, SEQ)
        kS = sb("kS", P, SEQ)
        dec = sb("dec", P, BATCH, NC)
        gate = sb("gate", P, BATCH, SEQ)
        gate_out = sb("gate_out", P, SEQ)
        act = [sb(f"act{n}", P, SEQ) for n in "qkv"]
        sq = [sb(f"sq{n}", P, SEQ) for n in "qk"]
        rn = [sb(f"rn{n}", P, SEQ) for n in "qk"]
        absz = sb("absz", P, SEQ)
        relz = sb("relz", P, SEQ)
        ez = sb("ez", P, SEQ)
        lz = sb("lz", P, SEQ)
        hz = sb("hz", P, SEQ)
        small = sb("small", P, SEQ, dt=U32)
        pre = sb("pre", P, SEQ)
        suf = sb("suf", P, SEQ)
        zero = sb("zero", P, SEQ)
        F = sb("F", P, LEV, SEQ)
        Fpre = sb("Fpre", P, SEQ)
        Fsuf = sb("Fsuf", P, SEQ)
        Pt = sb("Pt", P, 2, SEQ)
        Bt = sb("Bt", P, LEV, SEQ)
        T = sb("T", P, NC, P)
        Tt = sb("Tt", P, 2, NC, P)
        W = sb("W", P, LEV - 1, NC, P)
        kStok = sb("kStok", P, NC, P)
        vbT = sb("vbT", P, 2, NC, P)
        R = sb("R", P, 2, P)
        U = sb("U", P, 2, P)
        S = sb("S", P, 2, P)
        osq = sb("osq", P, SEQ)
        orn = sb("orn", P, SEQ)
        ogw = sb("ogw", P, SEQ)
        osc = sb("osc", P, SEQ)
        sg = sb("sg", P, 2, SEQ)

        LV = ctx.enter_context(nc.psum_tensor("LV", [P, 512], F32))
        IA = ctx.enter_context(nc.psum_tensor("IA", [P, 512], F32))
        IB = ctx.enter_context(nc.psum_tensor("IB", [P, 512], F32))
        CH_ = ctx.enter_context(nc.psum_tensor("CH", [P, 512], F32))
        OB = ctx.enter_context(nc.psum_tensor("OB", [P, 512], F32))
        FB = [ctx.enter_context(nc.psum_tensor(f"FB{n}", [P, 512], F32)) for n in range(3)]

        PER = {}

        def unit_sem(name, per=1):
            s = sem(name)
            PER[id(s)] = per
            keep.append(s)
            return s

        keep = []

        def after(eng, s, u, k=None):
            per = PER[id(s)]
            v = u * per + (per if k is None else k)
            if not isinstance(v, int) or v > 0:
                eng.wait_ge(s, v)

        d_const = sem("d_const")
        d_x = sem("d_x")
        d_pw = sem("d_pw")
        d_scr = sem("d_scr")
        d_out = sem("d_out")
        d_wp = sem("d_wp")
        d_wo = sem("d_wo")
        d_gu = sem("d_gu")
        d_dw = sem("d_dw")
        d_wbc = sem("d_wbc")
        d_bb = sem("d_bb")
        pro_v = sem("pro_v")
        pro_a = sem("pro_a")
        pro_p = sem("pro_p")
        end_v = sem("end_v")
        end_a = sem("end_a")

        m_g, m_go, m_q, m_k, m_v, m_nq, m_nk = [unit_sem(n) for n in
            ("m_g", "m_go", "m_q", "m_k", "m_v", "m_nq", "m_nk")]
        m_gate = unit_sem("m_gate", 2)
        m_up = unit_sem("m_up", 2)
        m_down = unit_sem("m_down", 4)
        m_lv = unit_sem("m_lv", LEV + 1)
        m_t1 = unit_sem("m_t1")
        m_tv = unit_sem("m_tv")
        m_tk = unit_sem("m_tk")
        m_w = unit_sem("m_w", 2 * (LEV - 1))
        m_t = unit_sem("m_t", 2 * (LEV - 1))
        m_tt = unit_sem("m_tt", 2 * (LEV - 2))
        m_r = unit_sem("m_r", NC - 1)
        m_u = unit_sem("m_u", NC)
        m_s = unit_sem("m_s", NC - 1)
        m_o = unit_sem("m_o", NC)
        m_ss = unit_sem("m_ss")
        m_wo = unit_sem("m_wo", 2)
        v_lv = unit_sem("v_lv", LEV + 1)
        v_t = unit_sem("v_t", 2 * LEV)
        v_sp = unit_sem("v_sp", 8)
        v_conv = [unit_sem(f"v_conv{n}", TAPS - 1) for n in "qkv"]
        v_norm = [unit_sem(f"v_norm{n}") for n in "qk"]
        v_prod = unit_sem("v_prod", LEV)
        v_full = unit_sem("v_full")
        v_r = unit_sem("v_r", NC - 1)
        v_s = unit_sem("v_s", NC - 1)
        v_h = unit_sem("v_h", 2)
        v_f = unit_sem("v_f", 4)
        v_og = unit_sem("v_og")
        v_osc = unit_sem("v_osc")
        v_sacc = unit_sem("v_sacc", 2)
        a_abs = unit_sem("a_abs", 2)
        a_e = unit_sem("a_e")
        a_ln = unit_sem("a_ln")
        a_gate = unit_sem("a_gate")
        a_tap = [unit_sem(f"a_tap{n}") for n in "qkv"]
        a_silu = [unit_sem(f"a_silu{n}") for n in "qkv"]
        a_nln = [unit_sem(f"a_nln{n}") for n in "qk"]
        a_rn = [unit_sem(f"a_rn{n}") for n in "qk"]
        a_F = unit_sem("a_F", LEV)
        a_full = unit_sem("a_full")
        a_tv = unit_sem("a_tv")
        a_tk = unit_sem("a_tk")
        a_gz = unit_sem("a_gz")
        a_w = unit_sem("a_w", 2 * (LEV - 1))
        a_t = unit_sem("a_t", 2 * (LEV - 2))
        a_u = unit_sem("a_u", NC)
        a_sg = unit_sem("a_sg", 2)
        a_osq = unit_sem("a_osq")
        a_oln = unit_sem("a_oln")
        a_orn = unit_sem("a_orn")
        p_sq = [unit_sem(f"p_sq{n}") for n in "qk"]
        p_zero = unit_sem("p_zero")
        p_sum = unit_sem("p_sum", 2 * LEV)
        p_kb = unit_sem("p_kb")
        p_vb = unit_sem("p_vb")
        p_h = unit_sem("p_h", 2)
        p_gate = unit_sem("p_gate")

        def halves(ap, s):
            return ap.rearrange("p (n two s) -> p n two s", two=2, s=s)

        def first(ap, s):
            return halves(ap, s)[:, :, 0, :]

        def second(ap, s):
            return halves(ap, s)[:, :, 1, :]

        def split(ap, s):
            return ap.rearrange("p (n s) -> p n s", s=s)

        def pair(ap, h):
            return ap[:, 2 * h:2 * h + 2, :].rearrange("p c n -> p (c n)")

        def c4(ap):
            return ap.rearrange("p (c n) -> p c n", c=NC)

        NCONST = 9 * 16
        PA_RSTD, PA_XT, PA_FAGA, PA_BETA = 2, 6, 10, 12
        PA_SGATE, PA_EXPR, PA_ROUTE = 16, 17, 19

        def sh_h(t):
            return sh_hidden[0:INNER, t * P:(t + 1) * P]

        def route_tok(t):
            return routed[:, t, :]

        sh_hidden = Bt[:, 0:2, :].rearrange("p a b -> p (a b)")
        sh_silu = Bt[:, 2:4, :].rearrange("p a b -> p (a b)")
        logits = Bt[:, 4, :].rearrange("p (t e) -> p t e", e=EXPERTS)
        lmask = Bt[:, 5, :].rearrange("p (t e) -> p t e", e=EXPERTS)
        routed = Bt[:, 6, :].rearrange("p (t e) -> p t e", e=EXPERTS)
        shg = R[:, 0, 0:TT]
        top8 = R[:, 1, 0:TT * 8].rearrange("p (t e) -> p t e", e=8)
        rsum = R[:, 1, 72:72 + TT]
        mean = R[:, 0, 8:8 + TT]
        var = R[:, 0, 16:16 + TT]
        rstd = R[:, 0, 24:24 + TT]
        PV_VAR, PV_XN, PV_SH, PV_ROUTE, PV_END = 5, 6, 8, 32, 37

        block = ctx.enter_context(nc.Block())

        @block.sync
        def _(sp):
            sp.dma_start(s_acc[:, :, :], x_in.rearrange("(t p) h -> p t h", p=P)).then_inc(d_x, 16)
            sp.dma_start(ident[:, :], consts[:, 0, :]).then_inc(d_const, 16)
            sp.dma_start(ones[:, :], consts[:, 1, :]).then_inc(d_const, 16)
            for c in range(NC):
                sp.dma_start(ident4[:, c, :], consts[:, 0, :]).then_inc(d_const, 16)
            sp.dma_start(mask[:, :, :], masks).then_inc(d_const, 16)
            sp.dma_start(onorm[:, :], o_norm).then_inc(d_const, 16)
            sp.dma_start(biases[:, :], consts[:, 2, 0:4]).then_inc(d_const, 16)
            sp.dma_start(F[:, 0, :].rearrange("p (k c) -> p k c", k=2), wab).then_inc(d_pw, 16)
            sp.dma_start(F[:, 1, 0:2 * (EXPERTS + 1)].rearrange("p (k c) -> p k c", k=2), wrouter).then_inc(d_pw, 16)
            sp.dma_start(F[:, 2, 0:2 * (P + HEADS)].rearrange("p (k c) -> p k c", k=2), wshared).then_inc(d_pw, 16)
            sp.dma_start(F[0:INNER, 3, 0:HID], wsh_down).then_inc(d_pw, 16)
            sp.dma_start(wpc[:, :], wproj[0:P, :]).then_inc(d_wp, 16)
            sp.wait_ge(pro_a, PA_BETA)
            sp.dma_start(beta_dram, KL[0:HEADS, 2:4, :].rearrange("p a b -> p (a b)")).then_inc(d_scr, 16)
            sp.wait_ge(pro_a, PA_ROUTE)
            sp.dma_start(route_dram, KL[0:EXPERTS, 0:2, :].rearrange("p a b -> p (a b)")).then_inc(d_scr, 16)
            sp.wait_ge(d_scr, 32)
            sp.dma_start(bb[:, :], beta_dram[0:1, 0:SEQ].to_broadcast([P, SEQ])).then_inc(d_bb, 16)

            def unit_loads(u, b, head, last):
                after(sp, m_up, u - 1)
                sp.dma_start(gu[:, :, :, :].rearrange("p k g c -> p (k g c)"),
                             wgu[bass.ds(u * P, P), :]).then_inc(d_gu, 16)
                after(sp, m_down, u - 1)
                sp.dma_start(dw[:, :], wdown[bass.ds(u * P, P), :]).then_inc(d_dw, 16)
                after(sp, p_h, u - 1)
                for e in range(2):
                    sp.dma_start(wbc[e * INNER:(e + 1) * INNER, :],
                                 route_dram[bass.ds(2 * u + e, 1), :].to_broadcast([INNER, TOK]))\
                        .then_inc(d_wbc, 16)
                if not last:
                    after(sp, p_kb, u)
                    after(sp, p_vb, u)
                    nh = head if b == 0 else head + 1
                    sp.dma_start(bb[:, :], beta_dram[bass.ds(nh, 1), (1 - b) * SEQ:(2 - b) * SEQ]
                                 .to_broadcast([P, SEQ])).then_inc(d_bb, 16)
                    if b == 0:
                        after(sp, m_v, u + 1)
                        after(sp, v_conv[2], u + 1)
                        after(sp, v_sp, u + 1)
                        sp.dma_start(wpc[:, :], wproj[bass.ds((head + 1) * P, P), :]).then_inc(d_wp, 16)
                if b == 0:
                    after(sp, m_wo, u - 1)
                    sp.dma_start(wo[:, :], wout[bass.ds(head * P, P), :]).then_inc(d_wo, 16)

            for b in range(BATCH):
                unit_loads(b, b, 0, False)
            with sp.Fori(1, HEADS - 1) as h:
                for b in range(BATCH):
                    unit_loads(2 * h + b, b, h, False)
            h = HEADS - 1
            for b in range(BATCH):
                u = 2 * h + b
                after(sp, m_up, u - 1)
                sp.dma_start(gu[:, :, :, :].rearrange("p k g c -> p (k g c)"),
                             wgu[u * P:(u + 1) * P, :]).then_inc(d_gu, 16)
                after(sp, m_down, u - 1)
                sp.dma_start(dw[:, :], wdown[u * P:(u + 1) * P, :]).then_inc(d_dw, 16)
                after(sp, p_h, u - 1)
                for e in range(2):
                    sp.dma_start(wbc[e * INNER:(e + 1) * INNER, :],
                                 route_dram[2 * u + e:2 * u + e + 1, :].to_broadcast([INNER, TOK])).then_inc(d_wbc, 16)
                if b == 0:
                    after(sp, p_kb, u)
                    after(sp, p_vb, u)
                    sp.dma_start(bb[:, :], beta_dram[h:h + 1, SEQ:2 * SEQ].to_broadcast([P, SEQ])).then_inc(d_bb, 16)
                    after(sp, m_wo, u - 1)
                    sp.dma_start(wo[:, :], wout[h * P:(h + 1) * P, :]).then_inc(d_wo, 16)
            after(sp, m_lv, UNITS - 1)
            sp.dma_start(KL[:, 0:4, :].rearrange("p a b -> p (a b)").rearrange("p (t h) -> p t h", t=TT),
                         x_in.rearrange("(t p) h -> p t h", p=P)).then_inc(d_x, 16)
            for t in range(4):
                sp.wait_ge(end_v, 2 * t + 2)
                sp.dma_start(out.rearrange("(t p) h -> p t h", p=P)[:, 2 * t:2 * t + 2, :],
                             s_acc[:, 2 * t:2 * t + 2, :]).then_inc(d_out, 16)
            sp.wait_ge(d_out, 64)

        @block.tensor
        def _(pe):
            mm = pe.matmul

            def proj(v, b, which, bank, ready):
                for k in range(KT):
                    m = mm(bank[:, :], wp[:, 2 * which + k, :], xT[:, k, b * SEQ:(b + 1) * SEQ],
                           start=k == 0, stop=k == KT - 1)
                m.then_inc(ready, 1)

            def prep_g(v, b, vh):
                pe.wait_ge(d_wp, vh * 16 + 16)
                after(pe, a_nln[1], v - 1)
                after(pe, a_oln, v - 3)
                mm(FB[0][:, :], wp[:, 6, :], fa[:, b * SEQ:(b + 1) * SEQ], start=True, stop=True).then_inc(m_g, 1)

            def prep_go(v, b):
                after(pe, a_tk, v - 2)
                after(pe, a_gz, v - 1)
                mm(FB[1][:, :], wp[:, 7, :], ga[:, b * SEQ:(b + 1) * SEQ], start=True, stop=True).then_inc(m_go, 1)

            def prep_q(v, b):
                after(pe, a_abs, v)
                proj(v, b, 0, FB[0], m_q)

            def prep_k(v, b):
                after(pe, v_conv[0], v)
                proj(v, b, 1, FB[0], m_k)

            def prep_v(v, b):
                after(pe, v_conv[1], v)
                proj(v, b, 2, FB[0], m_v)

            def prep_norm(v, n):
                after(pe, p_sq[n], v)
                if n == 0:
                    after(pe, v_conv[2], v)
                else:
                    after(pe, a_nln[0], v)
                mm(FB[0][:, :], ones[:, :], sq[n][:, :], start=True, stop=True).then_inc([m_nq, m_nk][n], 1)

            def level(u, n):
                if n == 0:
                    after(pe, v_norm[1], u)
                    after(pe, v_norm[0], u)
                    after(pe, v_lv, u - 1)
                else:
                    after(pe, v_lv, u, n)
                    after(pe, v_prod, u, n)
                out4 = LV[:, :].rearrange("p (w c i) -> p w c i", w=2, c=NC)
                for c in range(NC):
                    if n == 0:
                        m = mm(LV[:, c * CH:(c + 1) * CH], kn[:, c * CH:(c + 1) * CH],
                               qn[:, c * CH:(c + 1) * CH], start=True, stop=True)
                    else:
                        m = mm(out4[:, :, c, :], KL[:, (n - 1) % LRING, c * CH:(c + 1) * CH],
                               KQL[:, (n - 1) % LRING, :, c * (CH // 2):(c + 1) * (CH // 2)], start=True, stop=True)
                m.then_inc(m_lv, 1)

            def turn_first(u):
                after(pe, v_t, u - 1)
                after(pe, v_lv, u, 2)
                for c in range(NC):
                    m = pe.transpose(IB[:, c * P:(c + 1) * P], Bt[:, 0, c * CH:(c + 1) * CH], ident[:, :])
                m.then_inc(m_t1, 1)

            def turn_v(u, nxt):
                after(pe, p_vb, u)
                after(pe, v_h, u, 1)
                for c in range(NC):
                    m = pe.transpose(FB[2][:, c * P:(c + 1) * P], vb[:, c * CH:(c + 1) * CH], ident[:, :])
                m.then_inc(m_tv, 1)

            def turn_k(u):
                after(pe, v_full, u)
                after(pe, v_f, u, 3)
                for c in range(NC):
                    m = pe.transpose(FB[1][:, c * P:(c + 1) * P], kS[:, c * CH:(c + 1) * CH], ident[:, :])
                m.then_inc(m_tk, 1)

            def compact(bank, c, s):
                at = (c % 2) * (CH // 2)
                return bank[:, at:at + CH // 2].rearrange("p (n s) -> p n s", s=s)

            def inv_w(u, l):
                s = 1 << l
                after(pe, v_lv, u, l + 2)
                for h in range(2):
                    if l == 1:
                        after(pe, v_t, u, h + 1)
                    else:
                        after(pe, a_t, u, 2 * (l - 2) + h + 1)
                    for c in range(2 * h, 2 * h + 2):
                        m = mm(compact([IA, IB][h], c, s), Bt[:, l, c * CH:(c + 1) * CH],
                               halves(T[:, c, :], s)[:, :, 0, :], start=True, stop=True)
                    m.then_inc(m_w, 1)

            def inv_t(u, par, l):
                s = 1 << l
                for h in range(2):
                    after(pe, a_w, u, 2 * (l - 1) + h + 1)
                    for c in range(2 * h, 2 * h + 2):
                        m = mm(compact([IA, IB][h], c, s), W[:, l - 1, c, :],
                               halves(Tt[:, par, c, :], s)[:, :, 1, :], start=True, stop=True)
                    m.then_inc(m_t, 1)

            def turn_t(u, par, l):
                for h in range(2):
                    after(pe, v_t, u, 2 * l + h + 1)
                    for c in range(2 * h, 2 * h + 2):
                        m = pe.transpose([IA, IB][h][:, (2 + c % 2) * P:(3 + c % 2) * P], Tt[:, par, c, :], ident[:, :])
                    m.then_inc(m_tt, 1)

            def chain_r(w, par, c):
                after(pe, v_s, w, c)
                mm(CH_[:, 0:P], kbG[:, par, c * CH:(c + 1) * CH], S[:, c % 2, :], start=True, stop=True)\
                    .then_inc(m_r, 1)

            def chain_u(w, par, c):
                if c == 0:
                    after(pe, v_t, w)
                    after(pe, a_tv, w)
                    after(pe, v_sacc, w - 1)
                    rhs = vbT[:, par, 0, :]
                else:
                    after(pe, v_r, w, c)
                    rhs = R[:, c % 2, :]
                mm(CH_[:, P:2 * P], Tt[:, par, c, :], rhs, start=True, stop=True).then_inc(m_u, 1)

            def chain_so(w, par, c):
                after(pe, a_u, w, c + 1)
                if c == 0:
                    after(pe, a_tk, w)
                if c < NC - 1:
                    mm(CH_[:, 2 * P:3 * P], kStok[:, c, :], U[:, c % 2, :], start=True, stop=True).then_inc(m_s, 1)
                if c:
                    mm(OB[:, c * CH:(c + 1) * CH], S[:, c % 2, :], qG[:, par, c * CH:(c + 1) * CH],
                       start=True, stop=False)
                mm(OB[:, c * CH:(c + 1) * CH], U[:, c % 2, :], Pt[:, par, c * CH:(c + 1) * CH],
                   start=c == 0, stop=True).then_inc(m_o, 1)

            def gate_up(u, t, g, nxt, ks=range(KT)):
                if ks[0]:
                    pass
                elif (t, g) == (0, 0):
                    pe.wait_ge(d_gu, u * 16 + 16)
                    if nxt:
                        after(pe, a_gz, u + 1)
                    else:
                        after(pe, a_tk, u - 1)
                elif (t, g) == (0, 1):
                    after(pe, v_f, u - 1)
                elif (t, g) == (1, 0):
                    after(pe, a_sg, u, 1)
                else:
                    after(pe, a_tv, u)
                for k in ks:
                    m = mm(FB[1 + g][:, :], gu[:, k, g, :], xT[:, k, t * SEQ:(t + 1) * SEQ],
                           start=k == 0, stop=k == KT - 1)
                if ks[-1] == KT - 1:
                    m.then_inc([m_gate, m_up][g], 1)

            def down(u, j):
                if j == 0:
                    pe.wait_ge(d_dw, u * 16 + 16)
                    after(pe, a_sg, u, 2)
                elif j == 1:
                    after(pe, v_h, u, 2)
                else:
                    after(pe, v_f, u, j - 1)
                after(pe, p_h, u, j // 2 + 1)
                for t in range(2):
                    c = (2 * j + t) % 4
                    m = mm(FB[1 + j % 2][:, t * HID:(t + 1) * HID], sg[:, j // 2, c * P:(c + 1) * P], dw[:, :],
                           start=True, stop=True)
                m.then_inc(m_down, 1)

            def norm_out(w, v, nxt):
                after(pe, a_osq, w)
                if nxt:
                    after(pe, a_nln[1], v)
                else:
                    after(pe, a_oln, w - 1)
                mm(FB[0][:, :], ones[:, :], osq[:, :], start=True, stop=True).then_inc(m_ss, 1)

            def project_out(w, b, head, j):
                if b == 0 and j == 0:
                    pe.wait_ge(d_wo, head * 16 + 16)
                after(pe, v_osc, w)
                for t in range(2):
                    c = 2 * j + t
                    m = mm([CH_, OB][j][:, t * HID:(t + 1) * HID], osc[:, c * CH:(c + 1) * CH], wo[:, :],
                           start=True, stop=True)
                m.then_inc(m_wo, 1)

            def unit(u, b, head, w_head, old, nxt, nxt_head):
                w, v, par, other = u - 1, u + 1, b, 1 - b
                if nxt:
                    prep_g(v, other, nxt_head)
                level(u, 0)
                if nxt:
                    prep_go(v, other)
                if old:
                    chain_u(w, other, 0)
                level(u, 1)
                if old:
                    chain_so(w, other, 0)
                gate_up(u, 0, 0, nxt, (0,))
                turn_first(u)
                level(u, 2)
                if old:
                    chain_r(w, other, 1)
                if nxt:
                    prep_q(v, other)

                inv_w(u, 1)
                if old:
                    chain_u(w, other, 1)
                level(u, 3)
                inv_t(u, par, 1)
                if old:
                    chain_so(w, other, 1)
                gate_up(u, 0, 0, nxt, (1,))
                turn_t(u, par, 1)
                if old:
                    chain_r(w, other, 2)
                level(u, 4)

                inv_w(u, 2)
                if nxt:
                    prep_k(v, other)
                inv_t(u, par, 2)
                if old:
                    chain_u(w, other, 2)
                gate_up(u, 0, 1, nxt)
                turn_t(u, par, 2)
                if old:
                    chain_so(w, other, 2)
                level(u, 5)

                inv_w(u, 3)
                if nxt:
                    prep_v(v, other)
                inv_t(u, par, 3)
                if old:
                    chain_r(w, other, 3)
                gate_up(u, 1, 0, nxt)
                turn_t(u, par, 3)
                if old:
                    chain_u(w, other, 3)
                level(u, 6)

                inv_w(u, 4)
                turn_v(u, nxt)
                if old:
                    chain_so(w, other, 3)
                inv_t(u, par, 4)
                level(u, 7)
                turn_t(u, par, 4)
                if nxt:
                    prep_norm(v, 0)

                inv_w(u, 5)
                gate_up(u, 1, 1, nxt)
                inv_t(u, par, 5)
                down(u, 0)
                if nxt:
                    prep_norm(v, 1)
                turn_t(u, par, 5)
                inv_w(u, 6)
                if old:
                    norm_out(w, v, nxt)
                down(u, 1)
                inv_t(u, par, 6)
                down(u, 2)
                if old:
                    project_out(w, other, w_head, 0)
                    project_out(w, other, w_head, 1)
                down(u, 3)
                turn_k(u)

            pe.wait_ge(d_const, NCONST)
            pe.wait_ge(pro_v, PV_XN)
            for q in range(4):
                bank = ([LV, CH_, IA, IB])[q]
                for t in range(2):
                    for k in range(KT):
                        m = pe.transpose(bank[:, (k * 2 + t) * P:(k * 2 + t + 1) * P],
                                         f_acc[:, 2 * q + t, k * P:(k + 1) * P], ident[:, :])
                m.then_inc(pro_p, 1)
            pe.wait_ge(pro_a, PA_XT)
            pe.wait_ge(d_pw, 64)
            wab_sb = F[:, 0, :].rearrange("p (k c) -> p k c", k=2)
            for n in range(2):
                for b in range(2):
                    bank = (FB + [OB])[2 * n + b]
                    for k in range(KT):
                        m = mm(bank[:, :], wab_sb[:, k, n * P:(n + 1) * P], xT[:, k, b * SEQ:(b + 1) * SEQ],
                               start=k == 0, stop=k == 1)
                    m.then_inc(pro_p, 1)
            wsh = F[:, 2, 0:2 * (P + HEADS)].rearrange("p (k c) -> p k c", k=2)
            for b in range(2):
                for k in range(KT):
                    m = mm([IA, IB][b][0:HEADS, :], wsh[:, k, P:P + HEADS], xT[:, k, b * SEQ:(b + 1) * SEQ],
                           start=k == 0, stop=k == 1)
                m.then_inc(pro_p, 1)
            wr = F[:, 1, 0:2 * (EXPERTS + 1)].rearrange("p (k c) -> p k c", k=2)
            for q in range(2):
                for t in range(4):
                    for k in range(KT):
                        m = mm([LV, CH_][q][:, t * 80:t * 80 + EXPERTS + 1],
                               xT[:, k, (4 * q + t) * P:(4 * q + t + 1) * P], wr[:, k, :],
                               start=k == 0, stop=k == 1)
                m.then_inc(pro_p, 1)
            pe.wait_ge(pro_a, PA_FAGA)
            for b in range(2):
                for g in range(2):
                    for k in range(KT):
                        m = mm((FB + [OB])[2 * b + g][0:INNER, :], wsh[:, k, g * INNER:(g + 1) * INNER],
                               xT[:, k, b * SEQ:(b + 1) * SEQ], start=k == 0, stop=k == 1)
                m.then_inc(pro_p, 1)
            pe.wait_ge(pro_v, PV_SH)
            prep_g(0, 0, 0)
            prep_go(0, 0)
            for j in range(4):
                if j == 0:
                    pe.wait_ge(pro_a, PA_BETA)
                if j >= 2:
                    pe.wait_ge(pro_v, 33 + j - 2)
                for t in range(2):
                    tk = 2 * j + t
                    m = mm([IA, IB][j % 2][:, t * HID:(t + 1) * HID],
                           sh_h(tk), F[0:INNER, 3, 0:HID],
                           start=True, stop=True)
                m.then_inc(pro_p, 1)
            prep_q(0, 0)
            pe.wait_ge(pro_v, PV_ROUTE)
            pe.wait_ge(pro_a, PA_SGATE)
            for q in range(2):
                for t in range(4):
                    m = pe.transpose([LV, CH_][q][0:EXPERTS, t * P:(t + 1) * P], route_tok(4 * q + t), ident[:, :])
                m.then_inc(pro_p, 1)

            prep_k(0, 0)
            prep_v(0, 0)
            prep_norm(0, 0)
            prep_norm(0, 1)
            pe.wait_ge(pro_a, PA_ROUTE)
            unit(0, 0, 0, 0, False, True, 0)
            unit(1, 1, 0, 0, True, True, 1)
            with pe.Fori(1, HEADS - 1) as h:
                unit(2 * h, 0, h, h - 1, True, True, h)
                unit(2 * h + 1, 1, h, h, True, True, h + 1)
            unit(UNITS - 2, 0, HEADS - 1, HEADS - 2, True, True, HEADS - 1)
            unit(UNITS - 1, 1, HEADS - 1, HEADS - 1, True, False, 0)
            w = UNITS - 1
            for c in range(NC):
                if c:
                    chain_r(w, 1, c)
                chain_u(w, 1, c)
                chain_so(w, 1, c)
            norm_out(w, w + 1, False)
            project_out(w, 1, HEADS - 1, 0)
            project_out(w, 1, HEADS - 1, 1)

        @block.vector
        def _(ve):
            stt, ts, tt = ve.scalar_tensor_tensor, ve.tensor_scalar, ve.tensor_tensor

            def chained(ins, n):
                ins.then_inc(pro_v, 1)
                ve.wait_ge(pro_v, n)

            ve.wait_ge(d_x, 16)
            X = s_acc[:, :, :]
            chained(ve.tensor_reduce(mean, X, AX_X, ALU.add), 1)
            chained(ts(mean, mean, 1.0 / HID, None, ALU.mult), 2)
            chained(tt(s_acc[:, :, :], X, mean.unsqueeze(2).to_broadcast([P, TT, HID]), ALU.subtract), 3)
            chained(tt(f_acc[:, :, :], X, X, ALU.mult), 4)
            chained(ve.tensor_reduce(var, f_acc[:, :, :], AX_X, ALU.add), 5)
            ve.wait_ge(pro_a, PA_RSTD)
            chained(tt(f_acc[:, :, :], X, rstd.unsqueeze(2).to_broadcast([P, TT, HID]), ALU.mult), 6)
            ve.memset(s_acc[:, :, :], 0.0)
            ve.memset(zero[:, :], 0.0)
            ve.memset(W[:, :, :, :], 0.0)
            for b in range(2):
                ve.wait_ge(pro_p, 12 + b + 1)
                ve.wait_ge(pro_a, PA_BETA + b + 1)
                tt(sh_hidden[0:INNER, b * SEQ:(b + 1) * SEQ], sh_silu[0:INNER, b * SEQ:(b + 1) * SEQ],
                   (FB + [OB])[2 * b + 1][0:INNER, :], ALU.mult).then_inc(pro_v, 1)
            for q in range(2):
                ve.wait_ge(pro_p, 10 + q + 1)
                ve.tensor_copy(logits[:, 4 * q:4 * q + 4, :],
                               [LV, CH_][q][:, 0:320].rearrange("p (t e) -> p t e", e=80)[:, :, 0:EXPERTS]).then_inc(pro_v, 1)
            ve.wait_ge(pro_v, 10)
            for t in range(TT):
                ve.max(top8[:, t, :], logits[:, t, :]).then_inc(pro_v, 1)
            ve.wait_ge(pro_v, 18)
            for t in range(TT):
                ve.match_replace(lmask[:, t, :], top8[:, t, :], logits[:, t, :], NEG_BIG).then_inc(pro_v, 1)
            ve.wait_ge(pro_v, 26)
            chained(tt(lmask[:, :, :], lmask[:, :, :], logits[:, :, :], ALU.not_equal), 27)
            chained(tt(logits[:, :, :], logits[:, :, :], top8[:, :, 0:1].to_broadcast([P, TT, EXPERTS]),
                       ALU.subtract), 28)
            ve.wait_ge(pro_a, PA_EXPR)
            chained(tt(routed[:, :, :], lmask[:, :, :], logits[:, :, :], ALU.mult), 29)
            chained(ve.tensor_reduce(rsum, routed[:, :, :], AX_X, ALU.add), 30)
            chained(ve.reciprocal(rsum, rsum), 31)
            chained(tt(routed[:, :, :], routed[:, :, :], rsum.unsqueeze(2).to_broadcast([P, TT, EXPERTS]),
                       ALU.mult), 32)
            ve.wait_ge(pro_a, PA_SGATE)
            for j in range(4):
                ve.wait_ge(pro_p, 14 + j + 1)
                tt(f_acc[:, 2 * j:2 * j + 2, :], [IA, IB][j % 2][:, :].rearrange("p (t h) -> p t h", t=2),
                   shg[:, 2 * j:2 * j + 2].unsqueeze(2).to_broadcast([P, 2, HID]), ALU.mult).then_inc(pro_v, 1)

            def softplus_series(v, n):
                if n == 0:
                    after(ve, a_e, v)
                    ts(hz[:, :], ez[:, :], -0.25, None, ALU.mult).then_inc(v_sp, 1)
                    return
                after(ve, v_sp, v, n)
                stt(hz[:, :], hz[:, :], (1.0 / 3, -0.5, 1.0)[n - 1], ez[:, :], ALU.add, ALU.mult).then_inc(v_sp, 1)

            def softplus_small(v):
                after(ve, a_ln, v)
                ts(small[:, :], ez[:, :], SMALL, None, ALU.is_lt).then_inc(v_sp, 1)

            def conv(v, n, j):
                if j == 1:
                    after(ve, a_tap[n], v)
                else:
                    after(ve, v_conv[n], v, j - 1)
                stt(act[n][:, j:SEQ], FB[0][:, 0:SEQ - j],
                    taps[:, n, TAPS - 1 - j:TAPS - j], act[n][:, j:SEQ], ALU.mult, ALU.add)\
                    .then_inc(v_conv[n], 1)

            def softplus_select(v):
                ve.copy_predicated(lz[:, :], small[:, :], hz[:, :]).then_inc(v_sp, 1)

            def softplus_rest(v):
                after(ve, v_sp, v, 6)
                after(ve, a_abs, v)
                tt(lz[:, :], lz[:, :], relz[:, :], ALU.add).then_inc(v_sp, 1)
                after(ve, v_sp, v, 7)
                after(ve, a_full, v - 1)
                after(ve, p_sum, v - 1)
                ts(pre[:, :], lz[:, :], exp_a[:, :], -1.0, ALU.mult, ALU.mult).then_inc(v_sp, 1)

            def normalise(v, n):
                after(ve, v_full, v - 1)
                after(ve, a_rn[n], v)
                tt([qn, kn][n][:, :], act[n][:, :], rn[n][:, :], ALU.mult).then_inc(v_norm[n], 1)

            def product(v, l):
                s = 1 << l
                if l == 0:
                    after(ve, v_norm[0], v)
                    after(ve, v_norm[1], v)
                    after(ve, p_kb, v)
                after(ve, a_F, v, l + 1)
                tt(first(KL[:, l % LRING, :], s), first(kn[:, :], s), first(F[:, l, :], s), ALU.mult)
                for w, src in enumerate((kb, qn)):
                    m = tt(KQL[:, l % LRING, w, :].rearrange("p (n s) -> p n s", s=s), halves(src[:, :], s)[:, :, 1, :],
                           halves(F[:, l, :], s)[:, :, 1, :], ALU.mult)
                m.then_inc(v_prod, 1)

            def full_products(v, b):
                after(ve, a_full, v)
                after(ve, m_tk, v - 1)
                tt(kbG[:, b, :], kb[:, :], Fpre[:, :], ALU.mult)
                tt(qG[:, b, :], qn[:, :], Fpre[:, :], ALU.mult)
                ve.tensor_copy(dec[:, b, :], c4(Fpre[:, :])[:, :, CH - 1])
                tt(kS[:, :], kn[:, :], Fsuf[:, :], ALU.mult).then_inc(v_full, 1)

            def level(u, par, n):
                after(ve, m_lv, u, n + 1)
                if n == 0:
                    tt(c4(Pt[:, par, :]), c4(LV[:, :]), ident4[:, :, :], ALU.mult).then_inc(v_lv, 1)
                    return
                after(ve, v_lv, u, n)
                l, bank = n - 1, LV
                s = 1 << l
                tt(second(Bt[:, l, :], s), split(bank[:, 0:HALF], s), split(mask[:, l, :], s), ALU.mult)
                ve.copy_predicated(second(Pt[:, par, :], s), split(mask[:, l, :].bitcast(U32), s),
                                   split(bank[:, HALF:SEQ], s)).then_inc(v_lv, 1)

            def first_inverse(u, par):
                after(ve, m_t1, u)
                after(ve, v_lv, u, 2)
                for h in range(2):
                    c = slice(2 * h, 2 * h + 2)
                    tt(T[:, c, :], ident4[:, c, :], c4(IB[:, :])[:, c, :], ALU.subtract)
                    tt(Tt[:, par, c, :], ident4[:, c, :], c4(Bt[:, 0, :])[:, c, :], ALU.subtract).then_inc(v_t, 1)

            def inverse(u, par, l):
                s = 1 << l
                for h in range(2):
                    bank = [IA, IB][h]
                    t2 = second(pair(Tt[:, par, :, :], h), s)
                    after(ve, m_t, u, 2 * (l - 1) + h + 1)
                    after(ve, v_t, u, 2 * (l - 1) + h + 1)
                    tt(t2, t2, split(bank[:, 0:P], s), ALU.subtract).then_inc(v_t, 1)

            def right_side(w, par, c):
                after(ve, m_r, w, c)
                after(ve, a_tv, w)
                tt(R[:, c % 2, :], vbT[:, par, c, :], CH_[:, 0:P], ALU.subtract).then_inc(v_r, 1)

            def state(w, par, c):
                after(ve, m_s, w, c + 1)
                if c == 0:
                    ve.tensor_copy(S[:, 1, :], CH_[:, 2 * P:3 * P]).then_inc(v_s, 1)
                    return
                after(ve, v_s, w, c)
                stt(S[:, (c + 1) % 2, :], S[:, c % 2, :], dec[:, par, c:c + 1], CH_[:, 2 * P:3 * P],
                    ALU.mult, ALU.add).then_inc(v_s, 1)

            def hidden(u, t):
                after(ve, a_sg, u, t + 1)
                after(ve, m_up, u, t + 1)
                tt(sg[:, t, :], sg[:, t, :], FB[2][:, :], ALU.mult).then_inc(v_h, 1)

            def add_down(u, j):
                after(ve, m_down, u, j + 1)
                f = f_acc[:, 2 * j:2 * j + 2, :].rearrange("p t h -> p (t h)")
                tt(f, f, FB[1 + j % 2][:, :], ALU.add).then_inc(v_f, 1)

            def gated(w):
                after(ve, a_osq, w)
                after(ve, p_gate, w)
                stt(ogw[:, :], OB[:, :], onorm[:, :], gate_out[:, :], ALU.mult, ALU.mult).then_inc(v_og, 1)

            def scaled(w):
                after(ve, a_orn, w)
                after(ve, v_og, w)
                tt(osc[:, :], ogw[:, :], orn[:, :], ALU.mult).then_inc(v_osc, 1)

            def add_out(w, b):
                for j in range(2):
                    after(ve, m_wo, w, j + 1)
                    t = 4 * b + 2 * j
                    a = s_acc[:, t:t + 2, :].rearrange("p t h -> p (t h)")
                    tt(a, a, [CH_, OB][j][:, :], ALU.add).then_inc(v_sacc, 1)

            def unit(u, b, old, nxt):
                w, v, par, other = u - 1, u + 1, b, 1 - b
                level(u, par, 0)
                product(u, 2)
                level(u, par, 1)
                if old:
                    state(w, other, 0)
                first_inverse(u, par)
                level(u, par, 2)
                if old:
                    right_side(w, other, 1)
                product(u, 3)

                level(u, par, 3)
                inverse(u, par, 1)
                if nxt:
                    conv(v, 0, 1)
                if old:
                    state(w, other, 1)
                if nxt:
                    softplus_series(v, 0)
                    conv(v, 0, 2)
                    softplus_series(v, 1)
                    conv(v, 0, 3)
                if old:
                    right_side(w, other, 2)
                level(u, par, 4)
                product(u, 4)
                if nxt:
                    softplus_series(v, 2)
                inverse(u, par, 2)
                if nxt:
                    conv(v, 1, 1)
                    softplus_series(v, 3)
                    softplus_small(v)
                    after(ve, v_sp, v, 5)
                    conv(v, 1, 2)
                if old:
                    state(w, other, 2)
                if nxt:
                    softplus_select(v)
                    conv(v, 1, 3)
                product(u, 5)
                if nxt:
                    softplus_rest(v)
                level(u, par, 5)
                inverse(u, par, 3)
                if old:
                    right_side(w, other, 3)
                hidden(u, 0)
                product(u, 6)
                if nxt:
                    conv(v, 2, 1)
                    conv(v, 2, 2)

                level(u, par, 6)
                inverse(u, par, 4)
                if nxt:
                    conv(v, 2, 3)

                level(u, par, 7)
                full_products(u, par)
                inverse(u, par, 5)
                hidden(u, 1)
                if old:
                    gated(w)
                if nxt:
                    normalise(v, 0)
                add_down(u, 0)
                if nxt:
                    normalise(v, 1)
                add_down(u, 1)
                if old:
                    scaled(w)
                inverse(u, par, 6)
                if nxt:
                    product(v, 0)
                add_down(u, 2)
                if old:
                    add_out(w, other)
                if nxt:
                    product(v, 1)
                add_down(u, 3)

            for n in range(4):
                softplus_series(0, n)
            softplus_small(0)
            after(ve, v_sp, 0, 5)
            conv(0, 0, 1)
            softplus_select(0)
            conv(0, 0, 2)
            conv(0, 0, 3)
            softplus_rest(0)
            conv(0, 1, 1)
            conv(0, 1, 2)
            conv(0, 1, 3)
            ve.wait_ge(pro_a, PA_ROUTE)
            ve.wait_ge(pro_p, 20)
            ve.memset(Bt[:, :, :], 0.0)
            for j in (1, 2, 3):
                conv(0, 2, j)
            ve.wait_ge(d_scr, 32)
            ve.memset(KL[:, :, :], 0.0).then_inc(pro_v, 1)
            ve.wait_ge(pro_v, PV_END)
            normalise(0, 0)
            normalise(0, 1)
            product(0, 0)
            product(0, 1)
            unit(0, 0, False, True)
            unit(1, 1, True, True)
            with ve.Fori(1, HEADS - 1) as h:
                unit(2 * h, 0, True, True)
                unit(2 * h + 1, 1, True, True)
            unit(UNITS - 2, 0, True, True)
            unit(UNITS - 1, 1, True, False)
            w = UNITS - 1
            state(w, 1, 0)
            for c in range(1, NC):
                right_side(w, 1, c)
                if c < NC - 1:
                    state(w, 1, c)
            gated(w)
            scaled(w)
            add_out(w, 1)
            ve.wait_ge(d_x, 32)
            xr = KL[:, 0:4, :].rearrange("p a b -> p (a b)").rearrange("p (t h) -> p t h", t=TT)
            after(ve, v_sacc, UNITS - 1)
            for t in range(4):
                c = slice(2 * t, 2 * t + 2)
                ve.wait_ge(end_a, t + 1)
                tt(s_acc[:, c, :], s_acc[:, c, :], f_acc[:, c, :], ALU.mult).then_inc(end_v, 1)
                ve.wait_ge(end_v, 2 * t + 1)
                tt(s_acc[:, c, :], s_acc[:, c, :], xr[:, c, :], ALU.add).then_inc(end_v, 1)

        @block.scalar
        def _(ac):
            A = ac.activation
            LOGEXP = "natural_log_exp_and_others"
            eps, lscale, ln_eps, one = [biases[:, n:n + 1] for n in range(4)]

            def decay_in(v, vh):
                ac.wait_ge(d_wp, vh * 16 + 16)
                after(ac, m_g, v)
                after(ac, v_sp, v - 1)
                A(absz[:, :], FB[0][:, :], ACT.Abs, bias=dtb).then_inc(a_abs, 1)
                A(relz[:, :], FB[0][:, :], ACT.Relu, bias=dtb).then_inc(a_abs, 1)

            def decay_log(v):
                after(ac, a_abs, v, 1)
                A(ez[:, :], absz[:, :], ACT.Exp, scale=-1.0).then_inc(a_e, 1)
                A(exp_a[:, :], a_log, ACT.Exp)
                after(ac, a_e, v)
                A(lz[:, :], ez[:, :], ACT.Ln, bias=one).then_inc(a_ln, 1)

            def gate_in(v, vb_):
                after(ac, m_go, v)
                after(ac, p_gate, v - 2)
                A(gate[:, vb_, :], FB[1][:, :], ACT.Copy).then_inc(a_gz, 1)

            def gate_sigmoid(v, vb_):
                after(ac, a_gz, v)
                A(gate[:, vb_, :], gate[:, vb_, :], ACT.Sigmoid).then_inc(a_gate, 1)

            def tap(v, n):
                after(ac, [m_q, m_k, m_v][n], v)
                if n == 2:
                    after(ac, p_vb, v - 1)
                else:
                    after(ac, p_sq[n], v - 1)
                    after(ac, v_norm[n], v - 1)
                A(act[n][:, :], FB[0][:, :], ACT.Copy, scale=taps[:, n, TAPS - 1:TAPS]).then_inc(a_tap[n], 1)

            def silu(v, n):
                after(ac, v_conv[n], v)
                A(act[n][:, :], act[n][:, :], ACT.Silu).then_inc(a_silu[n], 1)

            def inv_norm(v, n):
                after(ac, [m_nq, m_nk][n], v)
                after(ac, v_norm[n], v - 1)
                A(rn[n][:, :], FB[0][:, :], ACT.Ln, bias=eps).then_inc(a_nln[n], 1)
                after(ac, a_nln[n], v)
                if n == 0:
                    A(rn[n][:, :], rn[n][:, :], ACT.Exp, scale=-0.5, bias=lscale).then_inc(a_rn[n], 1)
                else:
                    A(rn[n][:, :], rn[n][:, :], ACT.Exp, scale=-0.5).then_inc(a_rn[n], 1)

            def decay(v, l):
                s = 1 << l
                if l == 0:
                    after(ac, v_sp, v)
                    after(ac, p_zero, v)
                else:
                    after(ac, p_sum, v, 2 * l)
                after(ac, v_prod, v - 1, l + 1)
                A(halves(F[:, l, :], s)[:, :, 0, :], halves(suf[:, :], s)[:, :, 0, :], ACT.Exp)
                A(halves(F[:, l, :], s)[:, :, 1, :], halves(pre[:, :], s)[:, :, 1, :], ACT.Exp).then_inc(a_F, 1)

            def full_decay(v):
                after(ac, p_sum, v)
                after(ac, v_full, v - 1)
                A(Fpre[:, :], pre[:, :], ACT.Exp)
                A(Fsuf[:, :], suf[:, :], ACT.Exp).then_inc(a_full, 1)

            def copy_v(u, par):
                after(ac, m_tv, u)
                A(vbT[:, par, :, :], c4(FB[2][:, :]), ACT.Copy).then_inc(a_tv, 1)

            def copy_k(u):
                after(ac, m_tk, u)
                after(ac, m_s, u - 1)
                A(kStok[:, :, :], c4(FB[1][:, :]), ACT.Copy).then_inc(a_tk, 1)

            def copy_w(u, l):
                for h in range(2):
                    after(ac, m_w, u, 2 * (l - 1) + h + 1)
                    A(first(pair(W[:, l - 1, :, :], h), 1 << l), split([IA, IB][h][:, 0:P], 1 << l), ACT.Copy)\
                        .then_inc(a_w, 1)

            def copy_t(u, l):
                for h in range(2):
                    after(ac, m_tt, u, 2 * (l - 1) + h + 1)
                    A(first(pair(T[:, :, :], h), 1 << l), first([IA, IB][h][:, 2 * P:4 * P], 1 << l), ACT.Copy)\
                        .then_inc(a_t, 1)

            def copy_u(u, c):
                after(ac, m_u, u, c + 1)
                A(U[:, c % 2, :], CH_[:, P:2 * P], ACT.Copy).then_inc(a_u, 1)

            def silu_gate(u, t):
                after(ac, m_gate, u, t + 1)
                after(ac, m_down, u - 1)
                A(sg[:, t, :], FB[1][:, :], ACT.Silu).then_inc(a_sg, 1)

            def out_square(w):
                after(ac, m_o, w)
                A(osq[:, :], OB[:, :], ACT.Square).then_inc(a_osq, 1)

            def out_norm(w):
                after(ac, m_ss, w)
                after(ac, v_osc, w - 1)
                A(orn[:, :], FB[0][:, :], ACT.Ln, scale=1.0 / D, bias=eps).then_inc(a_oln, 1)
                after(ac, a_oln, w)
                A(orn[:, :], orn[:, :], ACT.Exp, scale=-0.5).then_inc(a_orn, 1)

            def unit(u, b, old, nxt, nxt_head):
                w, v, par, other = u - 1, u + 1, b, 1 - b
                if nxt:
                    decay_in(v, nxt_head)
                    gate_in(v, other)
                if old:
                    copy_u(w, 0)
                decay(u, 3)
                if nxt:
                    decay_log(v)
                decay(u, 4)
                if nxt:
                    tap(v, 0)

                copy_w(u, 1)
                if old:
                    copy_u(w, 1)
                decay(u, 5)
                copy_t(u, 1)

                copy_w(u, 2)
                decay(u, 6)
                if nxt:
                    tap(v, 1)
                if old:
                    copy_u(w, 2)
                full_decay(u)
                copy_t(u, 2)
                silu_gate(u, 0)

                if nxt:
                    silu(v, 0)
                copy_w(u, 3)
                if nxt:
                    gate_sigmoid(v, other)
                    tap(v, 2)
                copy_t(u, 3)
                if old:
                    copy_u(w, 3)

                copy_w(u, 4)
                if nxt:
                    silu(v, 1)
                silu_gate(u, 1)
                copy_v(u, par)
                copy_t(u, 4)
                if old:
                    out_square(w)

                copy_w(u, 5)
                if nxt:
                    silu(v, 2)
                ac.preload_act_table_set(LOGEXP)
                if nxt:
                    inv_norm(v, 0)
                copy_t(u, 5)
                if nxt:
                    inv_norm(v, 1)

                copy_w(u, 6)
                if nxt:
                    decay(v, 0)
                if old:
                    out_norm(w)
                if nxt:
                    decay(v, 1)
                copy_k(u)
                if nxt:
                    decay(v, 2)

            ac.preload_act_table_set(LOGEXP)
            ac.wait_ge(d_const, NCONST)
            ac.wait_ge(pro_v, PV_VAR)
            A(var, var, ACT.Ln, bias=ln_eps, scale=1.0 / HID).then_inc(pro_a, 1)
            ac.wait_ge(pro_a, 1)
            A(rstd, var, ACT.Exp, scale=-0.5).then_inc(pro_a, 1)
            for q in range(4):
                ac.wait_ge(pro_p, q + 1)
                A(xT[:, :, 2 * q * P:(2 * q + 2) * P], ([LV, CH_, IA, IB])[q][:, :].rearrange("p (k t) -> p k t", k=KT),
                  ACT.Copy).then_inc(pro_a, 1)
            for n in range(4):
                ac.wait_ge(pro_p, 5 + n)
                A([fa, ga][n // 2][:, (n % 2) * SEQ:(n % 2 + 1) * SEQ], (FB + [OB])[n][:, :], ACT.Copy).then_inc(pro_a, 1)
            for b in range(2):
                ac.wait_ge(pro_p, 9 + b)
                A(KL[0:HEADS, 2 + b, :], [IA, IB][b][0:HEADS, :], ACT.Sigmoid).then_inc(pro_a, 1)
            for b in range(2):
                ac.wait_ge(pro_p, 13 + b)
                A(sh_silu[0:INNER, b * SEQ:(b + 1) * SEQ], (FB + [OB])[2 * b][0:INNER, :], ACT.Silu).then_inc(pro_a, 1)
            ac.wait_ge(pro_v, 10)
            for q in range(2):
                A(shg[:, 4 * q:4 * q + 4], [LV, CH_][q][:, 0:320].rearrange("p (t e) -> p t e", e=80)[:, :, EXPERTS],
                  ACT.Sigmoid).then_inc(pro_a, 1)
            ac.wait_ge(pro_v, 28)
            A(logits[:, :, :], logits[:, :, :], ACT.Exp).then_inc(pro_a, 1)
            decay_in(0, 0)
            decay_log(0)
            gate_in(0, 0)
            tap(0, 0)
            for q in range(2):
                ac.wait_ge(pro_p, 19 + q)
                A(KL[0:EXPERTS, q, :], [LV, CH_][q][0:EXPERTS, :], ACT.Copy).then_inc(pro_a, 1)

            tap(0, 1)
            tap(0, 2)
            gate_sigmoid(0, 0)
            for n in range(3):
                silu(0, n)
            ac.preload_act_table_set(LOGEXP)
            inv_norm(0, 0)
            inv_norm(0, 1)
            for l in range(3):
                decay(0, l)
            unit(0, 0, False, True, 0)
            unit(1, 1, True, True, 1)
            with ac.Fori(1, HEADS - 1) as h:
                unit(2 * h, 0, True, True, h)
                unit(2 * h + 1, 1, True, True, h + 1)
            unit(UNITS - 2, 0, True, True, HEADS - 1)
            unit(UNITS - 1, 1, True, False, 0)
            for c in range(NC):
                copy_u(UNITS - 1, c)
            out_square(UNITS - 1)
            out_norm(UNITS - 1)
            after(ac, v_f, UNITS - 1)
            for t in range(4):
                c = slice(2 * t, 2 * t + 2)
                A(f_acc[:, c, :], f_acc[:, c, :], ACT.Silu).then_inc(end_a, 1)

        @block.gpsimd
        def _(gp):
            tt = gp.tensor_tensor

            def start_sums(v):
                after(gp, a_full, v - 1)
                tt(suf[:, :], zero[:, :], zero[:, :], ALU.add).then_inc(p_zero, 1)

            def merge(v, l):
                s = 1 << l
                after(gp, a_F, v, l + 1)
                after(gp, p_sum, v, 2 * l)
                if l == 0:
                    after(gp, p_zero, v)
                    after(gp, v_sp, v)
                sv, pv = halves(suf[:, :], s), halves(pre[:, :], s)
                n = SEQ // (2 * s)
                last = pv[:, :, :, s - 1:s]
                tt(sv[:, :, 0, :], sv[:, :, 0, :], last[:, :, 1, :].to_broadcast([P, n, s]), ALU.add).then_inc(p_sum, 1)
                after(gp, p_sum, v, 2 * l + 1)
                tt(pv[:, :, 1, :], pv[:, :, 1, :], last[:, :, 0, :].to_broadcast([P, n, s]), ALU.add).then_inc(p_sum, 1)

            def square(v, n):
                after(gp, a_silu[n], v)
                after(gp, [m_nq, m_nk][n], v - 1)
                tt(sq[n][:, :], act[n][:, :], act[n][:, :], ALU.mult).then_inc(p_sq[n], 1)

            def beta_v(v):
                gp.wait_ge(d_bb, v * 16 + 16)
                after(gp, a_silu[2], v)
                after(gp, m_tv, v - 1)
                tt(vb[:, :], act[2][:, :], bb[:, :], ALU.mult).then_inc(p_vb, 1)

            def beta_k(v):
                after(gp, v_norm[1], v)
                after(gp, v_full, v - 1)
                tt(kb[:, :], kn[:, :], bb[:, :], ALU.mult).then_inc(p_kb, 1)

            def weigh(u, t):
                gp.wait_ge(d_wbc, u * 32 + 32)
                after(gp, v_h, u, t + 1)
                tt(sg[:, t, :], sg[:, t, :], wbc[:, t * SEQ:(t + 1) * SEQ], ALU.mult).then_inc(p_h, 1)

            def hold_gate(u, par):
                after(gp, a_gate, u)
                after(gp, v_og, u - 1)
                tt(gate_out[:, :], gate[:, par, :], zero[:, :], ALU.add).then_inc(p_gate, 1)

            def unit(u, par, nxt):
                v = u + 1
                for l in (2, 3, 4, 5, 6):
                    merge(u, l)
                if nxt:
                    start_sums(v)
                    square(v, 0)
                    square(v, 1)
                weigh(u, 0)
                if nxt:
                    beta_v(v)
                weigh(u, 1)
                if nxt:
                    merge(v, 0)
                    beta_k(v)
                    merge(v, 1)
                hold_gate(u, par)

            gp.wait_ge(pro_v, PV_SH)
            start_sums(0)
            square(0, 0)
            square(0, 1)
            beta_v(0)
            beta_k(0)
            merge(0, 0)
            merge(0, 1)
            unit(0, 0, True)
            unit(1, 1, True)
            with gp.Fori(1, HEADS - 1) as h:
                unit(2 * h, 0, True)
                unit(2 * h + 1, 1, True)
            unit(UNITS - 2, 0, True)
            unit(UNITS - 1, 1, False)


def kernel(**inputs):
    import concourse.bacc as _bacc
    from concourse.bass_utils import run_bass_kernel_spmd as _run

    g = {k.replace("L0_attn_", "").replace("L0_ffn_", ""): np.ascontiguousarray(v) for k, v in inputs.items()}

    def k_tiles(w):
        return w.reshape(KT, P, -1).transpose(1, 0, 2)

    def per_head(w):
        return w.reshape(KT, P, HEADS, D).transpose(2, 1, 0, 3)

    def head_cols(w, n):
        return w.reshape(HEADS, D, n)

    heads = [per_head(g["Wq"]), per_head(g["Wk"]), per_head(g["Wv"]),
             g["Wfb"].reshape(P, HEADS, 1, D).transpose(1, 0, 2, 3), g["Wgb"].reshape(P, HEADS, 1, D).transpose(1, 0, 2, 3)]
    wproj = np.concatenate(
        [np.concatenate(heads, axis=2).reshape(HEADS, P, 8 * D), head_cols(g["conv_q_w"], TAPS),
         head_cols(g["conv_k_w"], TAPS), head_cols(g["conv_v_w"], TAPS), head_cols(g["dt_bias"], 1),
         np.broadcast_to(g["A_log"].reshape(HEADS, 1, 1), (HEADS, P, 1))], axis=2).reshape(HEADS * P, 8 * D + HC)
    guw = g["gu_w"].reshape(PAIRS, 2, 2, INNER, KT, P)
    consts = np.zeros((P, 3, P), np.float32)
    consts[:, 0] = np.eye(P, dtype=np.float32)
    consts[:, 1] = 1.0
    consts[:, 2, 0:4] = [NORM_EPS, -0.5 * np.log(D), LN_EPS, 1.0]
    masks = np.zeros((P, LEV, NC, CH // 2), np.float32)
    for l in range(LEV):
        s = 1 << l
        i = np.arange(CH).reshape(-1, 2, s)[:, 1].reshape(-1)
        j = np.arange(CH)[:, None]
        masks[:, l] = ((j // (2 * s) == i // (2 * s)) & (j % (2 * s) < s)).astype(np.float32)[:, None, :]
    arrays = {
        "x": g["hidden_states"].reshape(TOK, HID),
        "wproj": wproj,
        "wout": g["Wo"],
        "wab": k_tiles(np.concatenate([g["Wfa"], g["Wga"]], axis=1)),
        "wrouter": k_tiles(np.concatenate([g["gate_w"], g["sh_gate1_w"]], axis=0).T),
        "wshared": k_tiles(np.concatenate([g["sh_gate_w"].T, g["sh_up_w"].T, g["Wb"]], axis=1)),
        "wsh_down": g["sh_down_w"].T,
        "wgu": guw.transpose(0, 5, 4, 2, 1, 3).reshape(PAIRS * P, KT * 2 * P),
        "wdown": g["dp_w"].transpose(0, 2, 1).reshape(PAIRS * P, HID),
        "o_norm": g["o_norm_w"].reshape(P, 1),
        "consts": consts,
        "masks": masks.reshape(P, LEV, HALF),
    }
    arrays = {k: np.ascontiguousarray(v) for k, v in arrays.items()}
    nc = _bacc.Bacc("TRN2", target_bir_lowering=False, num_devices=1)
    aps = [nc.dram_tensor(k, v.shape, F32, kind="ExternalInput").ap() for k, v in arrays.items()]
    beta = nc.dram_tensor("beta_rows", [HEADS, TOK], F32, kind="Internal").ap()
    route = nc.dram_tensor("route_rows", [EXPERTS, TOK], F32, kind="Internal").ap()
    out = nc.dram_tensor("out", [TOK, HID], F32, kind="ExternalOutput").ap()
    build(nc, *aps, beta, route, out)
    r = _run(nc, [arrays], core_ids=[0])
    return r.results[0]["out"].reshape(BATCH, SEQ, HID)
```
